# Optimizing a Trainium2 kernel written in Bass

```python
import numpy as np
import jax
import jax.numpy as jnp

def _softmax(x, axis=-1):
    return jax.nn.softmax(x, axis=axis)

def _gelu(x):
    return jax.nn.gelu(x, approximate=True)

def _silu(x):
    return jax.nn.silu(x)

def _sigmoid(x):
    return jax.nn.sigmoid(x)

def _layernorm(x, axis=-1, eps=1e-05):
    m = jnp.mean(x, axis=axis, keepdims=True)
    v = jnp.var(x, axis=axis, keepdims=True)
    return (x - m) / jnp.sqrt(v + eps)

def _scatter_add(tgt, idx, src, axis=0):
    return tgt.at[idx].add(src)

def _segment_sum(src, seg, n):
    return jax.ops.segment_sum(src, seg, n)
kernel_name = 'mk_dlrm_tower_d1_rec_r8_baf3f6'

def setup_inputs(seed: int=0):
    np.random.seed(seed)
    _w = jnp.asarray

    def _rec_inputs():
        import jax
        import jax.numpy as jnp
        _tk = jax.random.key(seed)
        dense_ctx = jax.random.normal(jax.random.fold_in(_tk, 190), (512, 16), jnp.float32)
        ids = jnp.stack([jax.random.randint(jax.random.fold_in(_tk, 200 + f), (512,), 0, v, jnp.int32) for f, v in enumerate([125000, 1250, 125000, 125000, 1000, 1000, 1000, 12500, 125000, 125000, 125000, 1000, 1250, 12500, 125000, 125000, 1000, 1250, 12500, 1250, 1250, 1250, 12500, 125000, 12500, 12500, 1000, 1250, 1000, 12500, 1000, 1000, 125000, 125000, 1000, 1250, 125000, 12500, 12500])], axis=1)
        tbl_0 = 0.05 * jax.random.normal(jax.random.fold_in(_tk, 500 + 0), (125000, 16), jnp.float32)
        tbl_1 = 0.05 * jax.random.normal(jax.random.fold_in(_tk, 500 + 1), (1250, 16), jnp.float32)
        tbl_2 = 0.05 * jax.random.normal(jax.random.fold_in(_tk, 500 + 2), (125000, 16), jnp.float32)
        tbl_3 = 0.05 * jax.random.normal(jax.random.fold_in(_tk, 500 + 3), (125000, 16), jnp.float32)
        tbl_4 = 0.05 * jax.random.normal(jax.random.fold_in(_tk, 500 + 4), (1000, 16), jnp.float32)
        tbl_5 = 0.05 * jax.random.normal(jax.random.fold_in(_tk, 500 + 5), (1000, 16), jnp.float32)
        tbl_6 = 0.05 * jax.random.normal(jax.random.fold_in(_tk, 500 + 6), (1000, 16), jnp.float32)
        tbl_7 = 0.05 * jax.random.normal(jax.random.fold_in(_tk, 500 + 7), (12500, 16), jnp.float32)
        tbl_8 = 0.05 * jax.random.normal(jax.random.fold_in(_tk, 500 + 8), (125000, 16), jnp.float32)
        tbl_9 = 0.05 * jax.random.normal(jax.random.fold_in(_tk, 500 + 9), (125000, 16), jnp.float32)
        tbl_10 = 0.05 * jax.random.normal(jax.random.fold_in(_tk, 500 + 10), (125000, 16), jnp.float32)
        tbl_11 = 0.05 * jax.random.normal(jax.random.fold_in(_tk, 500 + 11), (1000, 16), jnp.float32)
        tbl_12 = 0.05 * jax.random.normal(jax.random.fold_in(_tk, 500 + 12), (1250, 16), jnp.float32)
        tbl_13 = 0.05 * jax.random.normal(jax.random.fold_in(_tk, 500 + 13), (12500, 16), jnp.float32)
        tbl_14 = 0.05 * jax.random.normal(jax.random.fold_in(_tk, 500 + 14), (125000, 16), jnp.float32)
        tbl_15 = 0.05 * jax.random.normal(jax.random.fold_in(_tk, 500 + 15), (125000, 16), jnp.float32)
        tbl_16 = 0.05 * jax.random.normal(jax.random.fold_in(_tk, 500 + 16), (1000, 16), jnp.float32)
        tbl_17 = 0.05 * jax.random.normal(jax.random.fold_in(_tk, 500 + 17), (1250, 16), jnp.float32)
        tbl_18 = 0.05 * jax.random.normal(jax.random.fold_in(_tk, 500 + 18), (12500, 16), jnp.float32)
        tbl_19 = 0.05 * jax.random.normal(jax.random.fold_in(_tk, 500 + 19), (1250, 16), jnp.float32)
        tbl_20 = 0.05 * jax.random.normal(jax.random.fold_in(_tk, 500 + 20), (1250, 16), jnp.float32)
        tbl_21 = 0.05 * jax.random.normal(jax.random.fold_in(_tk, 500 + 21), (1250, 16), jnp.float32)
        tbl_22 = 0.05 * jax.random.normal(jax.random.fold_in(_tk, 500 + 22), (12500, 16), jnp.float32)
        tbl_23 = 0.05 * jax.random.normal(jax.random.fold_in(_tk, 500 + 23), (125000, 16), jnp.float32)
        tbl_24 = 0.05 * jax.random.normal(jax.random.fold_in(_tk, 500 + 24), (12500, 16), jnp.float32)
        tbl_25 = 0.05 * jax.random.normal(jax.random.fold_in(_tk, 500 + 25), (12500, 16), jnp.float32)
        tbl_26 = 0.05 * jax.random.normal(jax.random.fold_in(_tk, 500 + 26), (1000, 16), jnp.float32)
        tbl_27 = 0.05 * jax.random.normal(jax.random.fold_in(_tk, 500 + 27), (1250, 16), jnp.float32)
        tbl_28 = 0.05 * jax.random.normal(jax.random.fold_in(_tk, 500 + 28), (1000, 16), jnp.float32)
        tbl_29 = 0.05 * jax.random.normal(jax.random.fold_in(_tk, 500 + 29), (12500, 16), jnp.float32)
        tbl_30 = 0.05 * jax.random.normal(jax.random.fold_in(_tk, 500 + 30), (1000, 16), jnp.float32)
        tbl_31 = 0.05 * jax.random.normal(jax.random.fold_in(_tk, 500 + 31), (1000, 16), jnp.float32)
        tbl_32 = 0.05 * jax.random.normal(jax.random.fold_in(_tk, 500 + 32), (125000, 16), jnp.float32)
        tbl_33 = 0.05 * jax.random.normal(jax.random.fold_in(_tk, 500 + 33), (125000, 16), jnp.float32)
        tbl_34 = 0.05 * jax.random.normal(jax.random.fold_in(_tk, 500 + 34), (1000, 16), jnp.float32)
        tbl_35 = 0.05 * jax.random.normal(jax.random.fold_in(_tk, 500 + 35), (1250, 16), jnp.float32)
        tbl_36 = 0.05 * jax.random.normal(jax.random.fold_in(_tk, 500 + 36), (125000, 16), jnp.float32)
        tbl_37 = 0.05 * jax.random.normal(jax.random.fold_in(_tk, 500 + 37), (12500, 16), jnp.float32)
        tbl_38 = 0.05 * jax.random.normal(jax.random.fold_in(_tk, 500 + 38), (12500, 16), jnp.float32)
        _rk = jax.random.fold_in(_tk, 7)
        W_top1 = 0.0606339 * jax.random.normal(jax.random.fold_in(_tk, 801), (272, 512), jnp.float32)
        W_top2 = 0.0441942 * jax.random.normal(jax.random.fold_in(_tk, 802), (512, 256), jnp.float32)
        W_top3 = 0.0625 * jax.random.normal(jax.random.fold_in(_tk, 803), (256, 1), jnp.float32)
        b_top1 = jnp.zeros((512,), jnp.float32)
        b_top2 = jnp.zeros((256,), jnp.float32)
        return (dense_ctx, ids, tbl_0, tbl_1, tbl_2, tbl_3, tbl_4, tbl_5, tbl_6, tbl_7, tbl_8, tbl_9, tbl_10, tbl_11, tbl_12, tbl_13, tbl_14, tbl_15, tbl_16, tbl_17, tbl_18, tbl_19, tbl_20, tbl_21, tbl_22, tbl_23, tbl_24, tbl_25, tbl_26, tbl_27, tbl_28, tbl_29, tbl_30, tbl_31, tbl_32, tbl_33, tbl_34, tbl_35, tbl_36, tbl_37, tbl_38, W_top1, b_top1, W_top2, b_top2, W_top3)
    dense_ctx, ids, tbl_0, tbl_1, tbl_2, tbl_3, tbl_4, tbl_5, tbl_6, tbl_7, tbl_8, tbl_9, tbl_10, tbl_11, tbl_12, tbl_13, tbl_14, tbl_15, tbl_16, tbl_17, tbl_18, tbl_19, tbl_20, tbl_21, tbl_22, tbl_23, tbl_24, tbl_25, tbl_26, tbl_27, tbl_28, tbl_29, tbl_30, tbl_31, tbl_32, tbl_33, tbl_34, tbl_35, tbl_36, tbl_37, tbl_38, W_top1, b_top1, W_top2, b_top2, W_top3 = _rec_inputs()

    def _L0_rec_setup():
        import jax, jax.numpy as jnp
        import numpy as np
        NUM_FIELD = 39
        CIN_SIZE = [128, 128]
        EMBED_DIM = 16
        BATCH = 256
        key = jax.random.key(seed)
        k1, k2, k3 = jax.random.split(key, 3)
        x_emb = jax.random.normal(k1, (BATCH, NUM_FIELD, EMBED_DIM), dtype=jnp.float32)
        W0 = jax.random.normal(k2, (CIN_SIZE[0], NUM_FIELD * NUM_FIELD), dtype=jnp.float32) * 0.02
        W1 = jax.random.normal(k3, (CIN_SIZE[1], CIN_SIZE[0] * NUM_FIELD), dtype=jnp.float32) * 0.02
        return {'x_emb': x_emb, 'W0': W0, 'W1': W1}
    _L0_rec_all = _L0_rec_setup()
    _L0_rec_in = {k: v for k, v in _L0_rec_all.items() if k in ('W0', 'W1')}
    del _L0_rec_all
    return {'dense_ctx': dense_ctx, 'ids': ids, 'tbl_0': tbl_0, 'tbl_1': tbl_1, 'tbl_2': tbl_2, 'tbl_3': tbl_3, 'tbl_4': tbl_4, 'tbl_5': tbl_5, 'tbl_6': tbl_6, 'tbl_7': tbl_7, 'tbl_8': tbl_8, 'tbl_9': tbl_9, 'tbl_10': tbl_10, 'tbl_11': tbl_11, 'tbl_12': tbl_12, 'tbl_13': tbl_13, 'tbl_14': tbl_14, 'tbl_15': tbl_15, 'tbl_16': tbl_16, 'tbl_17': tbl_17, 'tbl_18': tbl_18, 'tbl_19': tbl_19, 'tbl_20': tbl_20, 'tbl_21': tbl_21, 'tbl_22': tbl_22, 'tbl_23': tbl_23, 'tbl_24': tbl_24, 'tbl_25': tbl_25, 'tbl_26': tbl_26, 'tbl_27': tbl_27, 'tbl_28': tbl_28, 'tbl_29': tbl_29, 'tbl_30': tbl_30, 'tbl_31': tbl_31, 'tbl_32': tbl_32, 'tbl_33': tbl_33, 'tbl_34': tbl_34, 'tbl_35': tbl_35, 'tbl_36': tbl_36, 'tbl_37': tbl_37, 'tbl_38': tbl_38, 'W_top1': W_top1, 'b_top1': b_top1, 'W_top2': W_top2, 'b_top2': b_top2, 'W_top3': W_top3, 'L0_rec_W0': _L0_rec_in['W0'], 'L0_rec_W1': _L0_rec_in['W1']}

def reference(dense_ctx, ids, tbl_0, tbl_1, tbl_2, tbl_3, tbl_4, tbl_5, tbl_6, tbl_7, tbl_8, tbl_9, tbl_10, tbl_11, tbl_12, tbl_13, tbl_14, tbl_15, tbl_16, tbl_17, tbl_18, tbl_19, tbl_20, tbl_21, tbl_22, tbl_23, tbl_24, tbl_25, tbl_26, tbl_27, tbl_28, tbl_29, tbl_30, tbl_31, tbl_32, tbl_33, tbl_34, tbl_35, tbl_36, tbl_37, tbl_38, W_top1, b_top1, W_top2, b_top2, W_top3, L0_rec_W0, L0_rec_W1):
    import jax
    import jax.numpy as jnp

    def _L0_rec_ref(x_emb, W0, W1):
        import jax, jax.numpy as jnp
        import numpy as np
        NUM_FIELD = 39
        CIN_SIZE = [128, 128]
        EMBED_DIM = 16
        BATCH = 256
        B, F, D = x_emb.shape
        x = x_emb
        outs = []
        for W in (W0, W1):
            last = x.shape[1]
            inter = (x[:, :, None, :] * x_emb[:, None, :, :]).reshape(B, last * F, D)
            x = jnp.einsum('bid,hi->bhd', inter, W)
            outs.append(x.sum(axis=-1))
        return jnp.concatenate(outs, axis=-1)
    e = jnp.stack([tbl_0[ids[:, 0]], tbl_1[ids[:, 1]], tbl_2[ids[:, 2]], tbl_3[ids[:, 3]], tbl_4[ids[:, 4]], tbl_5[ids[:, 5]], tbl_6[ids[:, 6]], tbl_7[ids[:, 7]], tbl_8[ids[:, 8]], tbl_9[ids[:, 9]], tbl_10[ids[:, 10]], tbl_11[ids[:, 11]], tbl_12[ids[:, 12]], tbl_13[ids[:, 13]], tbl_14[ids[:, 14]], tbl_15[ids[:, 15]], tbl_16[ids[:, 16]], tbl_17[ids[:, 17]], tbl_18[ids[:, 18]], tbl_19[ids[:, 19]], tbl_20[ids[:, 20]], tbl_21[ids[:, 21]], tbl_22[ids[:, 22]], tbl_23[ids[:, 23]], tbl_24[ids[:, 24]], tbl_25[ids[:, 25]], tbl_26[ids[:, 26]], tbl_27[ids[:, 27]], tbl_28[ids[:, 28]], tbl_29[ids[:, 29]], tbl_30[ids[:, 30]], tbl_31[ids[:, 31]], tbl_32[ids[:, 32]], tbl_33[ids[:, 33]], tbl_34[ids[:, 34]], tbl_35[ids[:, 35]], tbl_36[ids[:, 36]], tbl_37[ids[:, 37]], tbl_38[ids[:, 38]]], axis=1)
    z = _L0_rec_ref(e, L0_rec_W0, L0_rec_W1)
    z = z.reshape(z.shape[0], -1)
    h = jnp.concatenate([z, dense_ctx], axis=1)
    h = jnp.maximum(h @ W_top1 + b_top1, 0.0)
    h = jnp.maximum(h @ W_top2 + b_top2, 0.0)
    y = h @ W_top3
    return y

_drawn_inputs = setup_inputs


def setup_inputs(seed=0):
    import zlib

    import numpy as np

    out = dict(_drawn_inputs(seed))
    spreads = {'b_top1': (0.0, 0.1), 'b_top2': (0.0, 0.1)}
    factors = {'tbl_0': 8.0,
     'tbl_1': 8.0,
     'tbl_2': 8.0,
     'tbl_3': 8.0,
     'tbl_4': 8.0,
     'tbl_5': 8.0,
     'tbl_6': 8.0,
     'tbl_7': 8.0,
     'tbl_8': 8.0,
     'tbl_9': 8.0,
     'tbl_10': 8.0,
     'tbl_11': 8.0,
     'tbl_12': 8.0,
     'tbl_13': 8.0,
     'tbl_14': 8.0,
     'tbl_15': 8.0,
     'tbl_16': 8.0,
     'tbl_17': 8.0,
     'tbl_18': 8.0,
     'tbl_19': 8.0,
     'tbl_20': 8.0,
     'tbl_21': 8.0,
     'tbl_22': 8.0,
     'tbl_23': 8.0,
     'tbl_24': 8.0,
     'tbl_25': 8.0,
     'tbl_26': 8.0,
     'tbl_27': 8.0,
     'tbl_28': 8.0,
     'tbl_29': 8.0,
     'tbl_30': 8.0,
     'tbl_31': 8.0,
     'tbl_32': 8.0,
     'tbl_33': 8.0,
     'tbl_34': 8.0,
     'tbl_35': 8.0,
     'tbl_36': 8.0,
     'tbl_37': 8.0,
     'tbl_38': 8.0,
     'L0_rec_W1': 8.0}
    for name, (base, spread) in spreads.items():
        noise = np.random.default_rng([zlib.crc32(name.encode()), seed]).standard_normal(out[name].shape)
        drawn = base * np.exp(spread * noise) if base else spread * noise
        out[name] = jnp.asarray(drawn.astype(out[name].dtype))
    for name, factor in factors.items():
        out[name] = (out[name] * factor).astype(out[name].dtype)
    return out
```

```python
from contextlib import ExitStack

import numpy as np

import concourse.bass as bass
from concourse import mybir

F32 = mybir.dt.float32
F32R = mybir.dt.float32r
I32 = mybir.dt.int32
ALU = mybir.AluOpType
ACT = mybir.ActivationFunctionType

P = 128
B, F, D, H = 512, 39, 16, 128
M1, M2, DENSE = 512, 256, 16
TILES = B // P
CB = 512 // D
COLS = P // CB
NG, GB = 4, 8
GF = F + 1
CHUNKS = 6
LEFT = F * (F + 1) // 2 - CHUNKS * P
STEPS = 4
SLOTS = COLS * STEPS
SPLIT = 2 * F
PARTS = 3
PF = F // PARTS
LAST = STEPS - 1
LROWS = 96


def base_fields():
    extra = list(range(LEFT, LEFT + P - 3 * F))
    return [p % 32 for p in range(96)] + [32 + (p % 7) for p in range(21)] + extra


def pair_tables():
    base = base_fields()
    want = [CHUNKS * base.count(v) + (v < LEFT) for v in range(F)]
    out = [{v} | {(v + s) % F for s in range(1, F // 2 + 1)} for v in range(F)]
    while True:
        over = [v for v in range(F) if len(out[v]) > want[v]]
        if not over:
            break
        came, queue = {over[0]: None}, [over[0]]
        for v in queue:
            if len(out[v]) < want[v]:
                break
            for w in sorted(out[v]):
                if w not in came:
                    came[w] = v
                    queue.append(w)
        while came[v] is not None:
            out[came[v]].remove(v)
            out[v].add(came[v])
            v = came[v]
    left = {v: sorted(out[v] - {v})[0] for v in range(LEFT)}
    rest = {v: sorted(out[v] - ({left[v]} if v in left else set())) for v in range(F)}
    partner = [[rest[base[p]].pop(0) for p in range(P)] for _ in range(CHUNKS)]
    return partner, left


def t_uses(first):
    uses = ([] if first else [("xT", -1)]) + [("eT", q) for q in range(4)] + [("base", 0)]
    for c in range(COLS):
        if c > 0:
            uses.append(("xT", c - 1))
        if c + 1 < COLS:
            uses.append(("base", c + 1))
        if c == 1 and not first:
            uses.append(("zT", 0))
        uses.append(("tr", c))
    return uses


T_FIRST, T_LATER, T_END = t_uses(True), t_uses(False), [("xT", -1), ("zT", 0)]


def count(tile, per_tile, k):
    return k if tile is None else tile * per_tile + (per_tile + k)


def t_count(tile, use, end=False):
    if tile is None:
        return T_FIRST.index(use) + 1
    return tile * len(T_LATER) + (len(T_FIRST) + (T_END if end else T_LATER).index(use) + 1)


def build(nc, ids, dense_t, sel, ident, ones_col, w0a, w0b, w1, wt1, wt2, wt3, b1, b2, tables, out):
    ctx = ExitStack()
    with ctx:
        def sb(name, shape, dt=F32):
            return ctx.enter_context(nc.sbuf_tensor(name, shape, dt))

        def ps(name, shape):
            return ctx.enter_context(nc.psum_tensor(name, shape, F32))

        def sem(name):
            return ctx.enter_context(nc.semaphore(name))

        ids_sb = sb("ids_sb", [P, TILES * F], I32)
        idx = sb("idx", [P, F], I32)
        emb = sb("emb", [P, F * D])
        emb_split = sb("emb_split", [P, SPLIT, D])
        embT = sb("embT", [SPLIT, P, D], F32R)
        sel_r = sb("sel_r", [SPLIT, (CHUNKS + 2) * P], F32R)
        ident_sb = sb("ident_sb", [P, P])
        base_sb = sb("base_sb", [P, 2, 512])
        prod = sb("prod", [P, STEPS, 2, 512])
        prod_hi = sb("prod_hi", [P, STEPS, 2, 512], F32R)
        prod_lo = sb("prod_lo", [P, LAST, 2, 512], F32R)
        w0_hi = sb("w0_hi", [P, CHUNKS + 1, H], F32R)
        w0_lo = sb("w0_lo", [P, CHUNKS, H], F32R)
        w1_hl = sb("w1_hl", [P, F, 2, H], F32R)
        w1_raw = sb("w1_raw", [P, PF, H])
        x1_sb = sb("x1_sb", [P, 512])
        x1T_hi = sb("x1T_hi", [P, NG, H], F32R)
        x1T_lo = sb("x1T_lo", [P, NG, H], F32R)
        e_rows = sb("e_rows", [P, NG, SPLIT])
        e_diag = [sb(f"e_diag{i}", [P, NG, 2, GB, GF], F32R) for i in range(2)]
        ones_sb = sb("ones_sb", [P, GB])
        gram_hi = sb("gram_hi", [P, GF, P], F32R)
        gram_lo = sb("gram_lo", [P, GF, P], F32R)
        z2_part = sb("z2_part", [P, H])
        z2_rows = sb("z2_rows", [P, H])
        z1T = sb("z1T", [P, B])
        z2T = sb("z2T", [P, B])
        denseT = sb("denseT", [DENSE, B])
        wt1_sb = sb("wt1_sb", [P, 2, M1])
        wt1d_sb = sb("wt1d_sb", [DENSE, M1])
        wt2_sb = sb("wt2_sb", [P, M1 // P, M2])
        wt3_sb = sb("wt3_sb", [P, M2 // P])
        b1_sb = sb("b1_sb", [P, M1 // P])
        b2_sb = sb("b2_sb", [P, M2 // P])
        y_sb = sb("y_sb", [1, B])
        w0a_sb = prod[:, 0, :, :].rearrange("p a n -> p (a n)")[:, 0:(CHUNKS + 1) * H]
        w0b_sb = prod[:, 1, :, :].rearrange("p a n -> p (a n)")[:, 0:(CHUNKS + 1) * H]
        sel_sb = prod[0:SPLIT, 2, :, :].rearrange("p a n -> p (a n)")
        h1 = prod[:, 0:2, :, :].rearrange("p s a n -> p (s a) n")
        h2 = prod[:, 2, :, :]

        sel_ps = [ps(f"sel_ps{i}", [P, 2, 512]) for i in range(2)]
        x1_ps = ps("x1_ps", [P, 512])
        t_ps = ps("t_ps", [P, 512])
        g_ps = ps("g_ps", [P, 512])
        z_ps = ps("z_ps", [P, 512])

        ids_in = sem("ids_in")
        consts_in = sem("consts_in")
        w1_in = sem("w1_in")
        tower_in = sem("tower_in")
        idx_ready = sem("idx_ready")
        look_up_begun = sem("look_up_begun")
        looked_up = [sem(f"looked_up{p}") for p in range(PARTS)]
        sel_ready = sem("sel_ready")
        w0_sum = sem("w0_sum")
        w0_hi_done = sem("w0_hi_done")
        w0_ready = sem("w0_ready")
        w1_hi_done = sem("w1_hi_done")
        w1_lo_done = sem("w1_lo_done")
        diag_zero = sem("diag_zero")
        diag_ready = sem("diag_ready")
        emb_hi_done = sem("emb_hi_done")
        emb_lo_done = sem("emb_lo_done")
        t_full = sem("t_full")
        xT_hi_done = sem("xT_hi_done")
        t_free = sem("t_free")
        sel_done = sem("sel_done")
        mult_done = sem("mult_done")
        hi_done = sem("hi_done")
        lo_done = sem("lo_done")
        main_done = sem("main_done")
        x1_taken = sem("x1_taken")
        diag_in = [sem(f"diag_in{i}") for i in range(2)]
        g_done = sem("g_done")
        g_hi_done = sem("g_hi_done")
        g_taken = sem("g_taken")
        z_done = sem("z_done")
        z_part_done = sem("z_part_done")
        z_sum_done = sem("z_sum_done")
        z1_done = sem("z1_done")
        h1_ps_done = sem("h1_ps_done")
        h1_done = sem("h1_done")
        h2_ps_done = sem("h2_ps_done")
        h2_done = sem("h2_done")
        y_ps_done = sem("y_ps_done")
        y_done = sem("y_done")
        y_out = sem("y_out")

        block = ctx.enter_context(nc.Block())

        @block.sync
        def _(sp):
            sp.dma_start(ids_sb[:, :].rearrange("p (t f) -> p t f", f=F),
                         ids.rearrange("(t p) f -> p t f", p=P)).then_inc(ids_in, 16)
            sp.dma_start(sel_sb, sel).then_inc(consts_in, 16)
            sp.dma_start(w0a_sb, w0a).then_inc(consts_in, 16)
            sp.dma_start(w0b_sb, w0b).then_inc(consts_in, 16)
            sp.dma_start(ident_sb[:, :], ident).then_inc(consts_in, 16)
            sp.dma_start(ones_sb[:, :], ones_col).then_inc(consts_in, 16)
            for p in range(PARTS):
                if p > 0:
                    sp.wait_ge(w1_lo_done, p)
                sp.dma_start(w1_raw[:, :, :], w1[:, p * PF:(p + 1) * PF, :]).then_inc(w1_in, 16)
            sp.dma_start(denseT[:, :], dense_t).then_inc(tower_in, 16)
            sp.dma_start(wt1_sb[:, :, :], wt1[0:2 * P, :].rearrange("(k p) n -> p k n", p=P)).then_inc(tower_in, 16)
            sp.dma_start(wt1d_sb[:, :], wt1[2 * P:2 * P + DENSE, :]).then_inc(tower_in, 16)
            sp.dma_start(wt2_sb[:, :, :], wt2.rearrange("(k p) n -> p k n", p=P)).then_inc(tower_in, 16)
            sp.dma_start(wt3_sb[:, :], wt3).then_inc(tower_in, 16)
            sp.dma_start(b1_sb[:, :], b1).then_inc(tower_in, 16)
            sp.dma_start(b2_sb[:, :], b2).then_inc(tower_in, 16)
            sp.wait_ge(diag_ready, 2)

            def diagonals(tile):
                for c in range(COLS):
                    sp.wait_ge(t_free, t_count(tile, ("tr", c)))
                    for g in range(GB):
                        rows = slice(g * D, (g + 1) * D)
                        sp.dma_start(e_diag[c % 2][rows, :, :, g, 0:F].bitcast(F32),
                                     e_rows[rows, :, :].rearrange("p n (s f) -> p n s f", s=2),
                                     ).then_inc(diag_in[c % 2], 16)

            diagonals(None)
            with sp.Fori(0, TILES - 1) as u:
                diagonals(u)
            sp.wait_ge(y_done, 1)
            sp.dma_start(out, y_sb[:, :]).then_inc(y_out, 16)
            sp.wait_ge(y_out, 16)

        @block.gpsimd
        def _(pool):
            pool.wait_ge(ids_in, 16)

            def look_up(tile):
                first = 0 if tile is None else (tile + 1) * F
                for p in range(PARTS):
                    if tile is not None:
                        pool.wait_ge(emb_lo_done, tile * PARTS + (p + 1))
                    nc.gpsimd.tensor_copy(idx[:, p * PF:(p + 1) * PF],
                                          ids_sb[:, bass.ds(first + p * PF, PF)]).then_inc(idx_ready, 1)
                    pool.wait_ge(idx_ready, count(tile, PARTS, p + 1))
                    pool.sem_inc(look_up_begun, 1)
                    for f in range(p * PF, (p + 1) * PF):
                        pool.indirect_dma_start(
                            emb[:, f * D:(f + 1) * D], None, tables[f],
                            bass.IndirectOffsetOnAxis(ap=idx[:, f:f + 1], axis=0),
                        ).then_inc(looked_up[p], 16)

            look_up(None)
            with pool.Fori(0, TILES - 1) as u:
                look_up(u)

        @block.tensor
        def _(pe):
            def selector(c):
                return sel_r[:, c * P:(c + 1) * P]

            def column(c):
                return embT[:, c * CB:(c + 1) * CB, :].rearrange("p b d -> p (b d)")

            def t_turn(tile, use, end=False):
                if tile is not None or use != T_FIRST[0]:
                    pe.wait_ge(t_free, count_before(tile, use, end))

            def count_before(tile, use, end):
                if tile is None:
                    return T_FIRST.index(use)
                return tile * len(T_LATER) + (len(T_FIRST) + (T_END if end else T_LATER).index(use))

            def transpose_emb(tile, q):
                t_turn(tile, ("eT", q))
                if q == 0:
                    pe.wait_ge(emb_lo_done, count(tile, PARTS, PARTS))
                for k in range(4):
                    mm = nc.tensor.transpose(t_ps[0:SPLIT, k * P:(k + 1) * P], emb_split[:, :, 4 * q + k],
                                             ident_sb[:, :])
                mm.then_inc(t_full, 1)

            def base_rows(tile, c):
                t_turn(tile, ("base", c))
                nc.tensor.matmul(t_ps[:, :], selector(0), column(c), start=True, stop=True).then_inc(t_full, 1)

            def emb_rows(tile, c):
                t_turn(tile, ("tr", c))
                for g in range(NG):
                    b0 = c * CB + g * GB
                    mm = nc.tensor.transpose(
                        t_ps[:, g * SPLIT:(g + 1) * SPLIT],
                        embT[:, b0:b0 + GB, :].rearrange("p b d -> p (b d)").bitcast(F32),
                        ident_sb[0:SPLIT, 0:SPLIT])
                mm.then_inc(t_full, 1)

            def transpose_x1(tile, c, end=False):
                t_turn(tile, ("xT", c), end)
                pe.wait_ge(x1_taken, count(tile, COLS, c + 1))
                for g in range(NG):
                    mm = nc.tensor.transpose(t_ps[:, g * P:(g + 1) * P], x1_sb[:, g * P:(g + 1) * P],
                                             ident_sb[:, :])
                mm.then_inc(t_full, 1)

            def partners(tile, n):
                c, s = divmod(n, STEPS)
                if tile is not None or n >= 2:
                    pe.wait_ge(mult_done, count(tile, SLOTS, n - 1))
                if n == 0:
                    pe.wait_ge(t_free, t_count(tile, ("eT", 3)))
                    if tile is None:
                        pe.wait_ge(sel_ready, 1)
                if s < LAST:
                    for a in range(2):
                        mm = nc.tensor.matmul(sel_ps[s % 2][:, a, :], selector(1 + 2 * s + a), column(c),
                                              start=True, stop=True)
                else:
                    mm = nc.tensor.matmul(sel_ps[s % 2][0:LROWS, 0, :], selector(1 + CHUNKS)[:, 0:LROWS],
                                          column(c), start=True, stop=True)
                mm.then_inc(sel_done, 1)

            def main(tile, n):
                c, s = divmod(n, STEPS)
                if tile is None and n == 0:
                    pe.wait_ge(w0_ready, 1)
                if s == 0 and (tile is not None or c > 0):
                    pe.wait_ge(x1_taken, count(tile, COLS, c))
                pe.wait_ge(lo_done, count(tile, SLOTS, n + 1))
                if s < LAST:
                    for a in range(2):
                        k = 2 * s + a
                        hi, lo = prod_hi[:, s, a, :], prod_lo[:, s, a, :]
                        nc.tensor.matmul(x1_ps[:, :], w0_hi[:, k, :], hi, start=(k == 0), stop=False)
                        nc.tensor.matmul(x1_ps[:, :], w0_hi[:, k, :], lo, start=False, stop=False)
                        mm = nc.tensor.matmul(x1_ps[:, :], w0_lo[:, k, :], hi, start=False, stop=False)
                else:
                    mm = nc.tensor.matmul(x1_ps[:, :], w0_hi[0:LROWS, CHUNKS, :], prod_hi[0:LROWS, s, 0, :],
                                          start=False, stop=True)
                mm.then_inc(main_done, 1)

            def gram(tile, c, g, end=False):
                if g == 0:
                    pe.wait_ge(t_free, t_count(tile, ("xT", c), end))
                    if c < 0:
                        pe.wait_ge(diag_in[1], tile * (2 * 16 * GB) + 2 * 16 * GB)
                    else:
                        pe.wait_ge(diag_in[c % 2], count(tile, 2 * 16 * GB, 16 * GB * (c // 2 + 1)))
                if tile is not None or c > 0 or g > 0:
                    pe.wait_ge(g_taken, count(tile, SLOTS, NG * c + g))
                o = g_ps[:, 0:GB * GF]
                e_hi = e_diag[c % 2][:, g, 0, :, :].rearrange("p b f -> p (b f)")
                e_lo = e_diag[c % 2][:, g, 1, :, :].rearrange("p b f -> p (b f)")
                nc.tensor.matmul(o, x1T_hi[:, g, :], e_hi, start=True, stop=False)
                nc.tensor.matmul(o, x1T_hi[:, g, :], e_lo, start=False, stop=False)
                nc.tensor.matmul(o, x1T_lo[:, g, :], e_hi, start=False, stop=True).then_inc(g_done, 1)

            def layer2(tile, j0, j1):
                if j0 == 0:
                    pe.wait_ge(g_taken, count(tile, SLOTS, 0))
                for j in range(j0, j1):
                    w = w1_hl[:, j, :, :].rearrange("p s h -> p (s h)")
                    nc.tensor.matmul(z_ps[:, 0:2 * H], gram_hi[:, j, :], w, start=(j == 0), stop=False)
                    mm = nc.tensor.matmul(z_ps[:, 0:2 * H], gram_lo[:, j, :], w, start=False,
                                          stop=(j == F - 1))
                if j1 == F:
                    mm.then_inc(z_done, 1)

            def transpose_z2(tile, end=False):
                t_turn(tile, ("zT", 0), end)
                pe.wait_ge(z_sum_done, tile + 1)
                nc.tensor.transpose(t_ps[:, 0:P], z2_rows[:, :], ident_sb[:, :]).then_inc(t_full, 1)

            def do_tile(tile):
                later = tile is not None
                if later:
                    transpose_x1(tile, -1)
                    gram(tile, -1, 0)
                    gram(tile, -1, 1)
                transpose_emb(tile, 0)
                if later:
                    gram(tile, -1, 2)
                transpose_emb(tile, 1)
                if later:
                    gram(tile, -1, 3)
                transpose_emb(tile, 2)
                transpose_emb(tile, 3)
                partners(tile, 0)
                base_rows(tile, 0)
                partners(tile, 1)
                if later:
                    layer2(tile, 0, 15)
                for n in range(SLOTS):
                    c, s = divmod(n, STEPS)
                    if s == 3 and c > 0:
                        gram(tile, c - 1, 2)
                    if n + 2 < SLOTS:
                        partners(tile, n + 2)
                    main(tile, n)
                    if c == 0 and later:
                        layer2(tile, 15 + 6 * s, 15 + 6 * (s + 1))
                    if s == 0 and c > 0:
                        transpose_x1(tile, c - 1)
                    if s == 1:
                        if c > 0:
                            gram(tile, c - 1, 0)
                        if c + 1 < COLS:
                            base_rows(tile, c + 1)
                        if c == 1 and later:
                            transpose_z2(tile)
                    if s == 2:
                        if c > 0:
                            gram(tile, c - 1, 1)
                        emb_rows(tile, c)
                    if s == 3 and c > 0:
                        gram(tile, c - 1, 3)

            pe.wait_ge(consts_in, 80)
            do_tile(None)
            pe.wait_ge(w1_lo_done, PARTS)
            with pe.Fori(0, TILES - 1) as u:
                do_tile(u)
            end = TILES - 1
            transpose_x1(end, -1, True)
            for g in range(NG):
                gram(end, -1, g, True)
            layer2(end, 0, F)
            transpose_z2(end, True)

            pe.wait_ge(tower_in, 7 * 16)
            pe.wait_ge(t_free, t_count(end, ("zT", 0), True))
            for m in range(M1 // P):
                o = sel_ps[m // 2][:, m % 2, :]
                cols = slice(m * P, (m + 1) * P)
                nc.tensor.matmul(o, wt1_sb[:, 0, cols], z1T[:, :], start=True, stop=False)
                nc.tensor.matmul(o, wt1_sb[:, 1, cols], z2T[:, :], start=False, stop=False)
                nc.tensor.matmul(o, wt1d_sb[:, cols], denseT[:, :], start=False, stop=True).then_inc(h1_ps_done, 1)
            for m in range(M2 // P):
                o = [x1_ps, g_ps][m]
                for k in range(M1 // P):
                    pe.wait_ge(h1_done, k + 1)
                    mm = nc.tensor.matmul(o[:, :], wt2_sb[:, k, m * P:(m + 1) * P], h1[:, k, :],
                                          start=(k == 0), stop=(k == M1 // P - 1))
                mm.then_inc(h2_ps_done, 1)
            for k in range(M2 // P):
                pe.wait_ge(h2_done, k + 1)
                mm = nc.tensor.matmul(t_ps[0:1, :], wt3_sb[:, k:k + 1], h2[:, k, :],
                                      start=(k == 0), stop=(k == M2 // P - 1))
            mm.then_inc(y_ps_done, 1)

        @block.scalar
        def _(act):
            def copy(o, i):
                return nc.scalar.activation(o, i, ACT.Copy)

            def split_emb(tile):
                for p in range(PARTS):
                    act.wait_ge(looked_up[p], count(tile, 16 * PF, 16 * PF))
                    fields = slice(p * PF, (p + 1) * PF)
                    copy(emb_split[:, fields, :].bitcast(F32R),
                         emb[:, p * PF * D:(p + 1) * PF * D].rearrange("p (f d) -> p f d", d=D),
                         ).then_inc(emb_hi_done, 1)

            def take_embT(tile, q):
                act.wait_ge(t_full, t_count(tile, ("eT", q)))
                copy(embT[:, :, 4 * q:4 * q + 4].rearrange("p b d -> p d b"),
                     t_ps[0:SPLIT, :].rearrange("p (d b) -> p d b", d=4)).then_inc(t_free, 1)

            def take_base(tile, c):
                act.wait_ge(t_full, t_count(tile, ("base", c)))
                if tile is not None or c >= 2:
                    act.wait_ge(mult_done, count(tile, SLOTS, STEPS * (c - 1)))
                copy(base_sb[:, c % 2, :], t_ps[:, :]).then_inc(t_free, 1)

            def take_emb_rows(tile, c):
                act.wait_ge(t_full, t_count(tile, ("tr", c)))
                if tile is not None or c > 0:
                    if c % 2:
                        act.wait_ge(diag_in[0], count(tile, 2 * 16 * GB, 16 * GB * (c // 2 + 1)))
                    else:
                        act.wait_ge(diag_in[1], count(tile, 2 * 16 * GB, 16 * GB * (c // 2)))
                copy(e_rows[:, :, :].rearrange("p n f -> p (n f)"), t_ps[:, 0:NG * SPLIT]).then_inc(t_free, 1)

            def take_x1T(tile, c, end=False):
                act.wait_ge(t_full, t_count(tile, ("xT", c), end))
                copy(x1T_hi[:, :, :].rearrange("p n h -> p (n h)"), t_ps[:, :]).then_inc(xT_hi_done, 1)

            def products_hi(tile, n):
                s = n % STEPS
                act.wait_ge(mult_done, count(tile, SLOTS, n + 1))
                if tile is not None or n >= STEPS:
                    act.wait_ge(main_done, count(tile, SLOTS, n - STEPS + 1))
                if s < LAST:
                    copy(prod_hi[:, s, :, :], prod[:, s, :, :]).then_inc(hi_done, 1)
                else:
                    copy(prod_hi[0:LROWS, s, 0, :], prod[0:LROWS, s, 0, :]).then_inc(hi_done, 1)

            def take_x1(tile, c):
                act.wait_ge(main_done, count(tile, SLOTS, STEPS * (c + 1)))
                copy(x1_sb[:, :], x1_ps[:, :]).then_inc(x1_taken, 1)

            def take_gram(tile, c, g):
                act.wait_ge(g_done, count(tile, SLOTS, NG * c + g + 1))
                if tile is not None and c == 0 and g == 0:
                    act.wait_ge(z_done, tile + 1)
                    act.wait_ge(z1_done, tile + 1)
                b0 = (c % COLS) * CB + g * GB
                copy(gram_hi[:, :, b0:b0 + GB].rearrange("p j b -> p b j"),
                     g_ps[:, 0:GB * GF].rearrange("p (b j) -> p b j", b=GB)).then_inc(g_hi_done, 1)

            def take_z2(tile):
                act.wait_ge(z_done, tile + 1)
                copy(z2_part[:, :], z_ps[:, H:2 * H]).then_inc(z_part_done, 1)

            def do_tile(tile):
                later = tile is not None
                if later:
                    take_x1T(tile, -1)
                    take_gram(tile, -1, 0)
                    take_gram(tile, -1, 1)
                split_emb(tile)
                take_embT(tile, 0)
                if later:
                    take_gram(tile, -1, 2)
                take_embT(tile, 1)
                if later:
                    take_gram(tile, -1, 3)
                take_embT(tile, 2)
                take_embT(tile, 3)
                take_base(tile, 0)
                products_hi(tile, 0)
                for n in range(SLOTS):
                    c, s = divmod(n, STEPS)
                    if s == 3 and c > 0:
                        take_gram(tile, c - 1, 2)
                    if n + 1 < SLOTS:
                        products_hi(tile, n + 1)
                    if s == 0 and c > 0:
                        take_x1T(tile, c - 1)
                    if s == 0 and c == 1 and later:
                        take_z2(tile)
                    if s == 1:
                        if c > 0:
                            take_gram(tile, c - 1, 0)
                        if c + 1 < COLS:
                            take_base(tile, c + 1)
                    if s == 2:
                        if c > 0:
                            take_gram(tile, c - 1, 1)
                        take_emb_rows(tile, c)
                    if s == 3:
                        take_x1(tile, c)
                        if c > 0:
                            take_gram(tile, c - 1, 3)

            act.wait_ge(w0_sum, 1)
            copy(w0_hi[:, :, :].rearrange("p k h -> p (k h)"), w0a_sb).then_inc(w0_hi_done, 1)
            for p in range(PARTS):
                act.wait_ge(w1_in, 16 * (p + 1))
                copy(w1_hl[:, p * PF:(p + 1) * PF, 0, :], w1_raw[:, :, :]).then_inc(w1_hi_done, 1)
            do_tile(None)
            with act.Fori(0, TILES - 1) as u:
                do_tile(u)
            end = TILES - 1
            take_x1T(end, -1, True)
            for g in range(NG):
                take_gram(end, -1, g)
            take_z2(end)

            act.wait_ge(tower_in, 7 * 16)
            for m in range(M1 // P):
                act.wait_ge(h1_ps_done, m + 1)
                nc.scalar.activation(h1[:, m, :], sel_ps[m // 2][:, m % 2, :], ACT.Relu,
                                     bias=b1_sb[:, m:m + 1]).then_inc(h1_done, 1)
            for m in range(M2 // P):
                act.wait_ge(h2_ps_done, m + 1)
                nc.scalar.activation(h2[:, m, :], [x1_ps, g_ps][m][:, :], ACT.Relu,
                                     bias=b2_sb[:, m:m + 1]).then_inc(h2_done, 1)
            act.wait_ge(y_ps_done, 1)
            copy(y_sb[:, :], t_ps[0:1, :]).then_inc(y_done, 1)

        @block.vector
        def _(dve):
            def subtract(o, whole, hi):
                return nc.vector.tensor_tensor(o, whole, hi, ALU.subtract)

            def split_emb(tile):
                for p in range(PARTS):
                    dve.wait_ge(emb_hi_done, count(tile, PARTS, p + 1))
                    subtract(emb_split[:, F + p * PF:F + (p + 1) * PF, :],
                             emb[:, p * PF * D:(p + 1) * PF * D].rearrange("p (f d) -> p f d", d=D),
                             emb_split[:, p * PF:(p + 1) * PF, :]).then_inc(emb_lo_done, 1)

            def multiply(tile, n):
                c, s = divmod(n, STEPS)
                dve.wait_ge(sel_done, count(tile, SLOTS, n + 1))
                if s == 0:
                    dve.wait_ge(t_free, t_count(tile, ("base", c)))
                if tile is not None or n >= STEPS:
                    dve.wait_ge(hi_done, count(tile, SLOTS, n - STEPS + 1))
                if s < LAST:
                    base = base_sb[:, c % 2, :].unsqueeze(1).to_broadcast([P, 2, 512])
                    nc.vector.tensor_tensor(prod[:, s, :, :], sel_ps[s % 2][:, :, :], base,
                                            ALU.mult).then_inc(mult_done, 1)
                else:
                    nc.vector.tensor_tensor(prod[0:LROWS, s, 0, :], sel_ps[s % 2][0:LROWS, 0, :],
                                            base_sb[0:LROWS, c % 2, :], ALU.mult).then_inc(mult_done, 1)

            def products_lo(tile, n):
                s = n % STEPS
                dve.wait_ge(hi_done, count(tile, SLOTS, n + 1))
                if tile is not None or n >= STEPS:
                    dve.wait_ge(main_done, count(tile, SLOTS, n - STEPS + 1))
                if s < LAST:
                    subtract(prod_lo[:, s, :, :], prod[:, s, :, :],
                             prod_hi[:, s, :, :].bitcast(F32)).then_inc(lo_done, 1)
                else:
                    subtract(prod_hi[32:64, s, 0, :], prod[32:64, s, 0, :],
                             prod_hi[32:64, s, 0, :].bitcast(F32)).then_inc(lo_done, 1)

            def take_x1T(tile, c):
                dve.wait_ge(xT_hi_done, count(tile, COLS, c + 1))
                subtract(x1T_lo[:, :, :].rearrange("p n h -> p (n h)"), t_ps[:, :],
                         x1T_hi[:, :, :].rearrange("p n h -> p (n h)").bitcast(F32)).then_inc(t_free, 1)

            def take_gram(tile, c, g):
                dve.wait_ge(g_hi_done, count(tile, SLOTS, NG * c + g + 1))
                b0 = (c % COLS) * CB + g * GB
                subtract(gram_lo[:, :, b0:b0 + GB].rearrange("p j b -> p b j"),
                         g_ps[:, 0:GB * GF].rearrange("p (b j) -> p b j", b=GB),
                         gram_hi[:, :, b0:b0 + GB].rearrange("p j b -> p b j").bitcast(F32),
                         ).then_inc(g_taken, 1)

            def sum_z2(tile):
                dve.wait_ge(z_part_done, tile + 1)
                nc.vector.tensor_tensor(z2_rows[:, :], z_ps[:, 0:H], z2_part[:, :],
                                        ALU.add).then_inc(z_sum_done, 1)

            def take_z1(tile):
                dve.wait_ge(g_taken, count(tile, SLOTS, 0))
                nc.vector.tensor_tensor(z1T[:, bass.ds(tile * P, P)], gram_hi[:, F, :].bitcast(F32),
                                        gram_lo[:, F, :].bitcast(F32), ALU.add).then_inc(z1_done, 1)

            def take_z2T(tile, end=False):
                dve.wait_ge(t_full, t_count(tile, ("zT", 0), end))
                nc.vector.tensor_copy(z2T[:, bass.ds(tile * P, P)], t_ps[:, 0:P]).then_inc(t_free, 1)

            def do_tile(tile):
                later = tile is not None
                if later:
                    take_x1T(tile, -1)
                    take_gram(tile, -1, 0)
                    take_gram(tile, -1, 1)
                split_emb(tile)
                if later:
                    take_gram(tile, -1, 2)
                    take_gram(tile, -1, 3)
                multiply(tile, 0)
                multiply(tile, 1)
                products_lo(tile, 0)
                for n in range(SLOTS):
                    c, s = divmod(n, STEPS)
                    if s == 3 and c > 0:
                        take_gram(tile, c - 1, 2)
                    if n + 2 < SLOTS:
                        multiply(tile, n + 2)
                    if n + 1 < SLOTS:
                        products_lo(tile, n + 1)
                    if s == 0 and c > 0:
                        take_x1T(tile, c - 1)
                    if s == 0 and c == 1 and later:
                        sum_z2(tile)
                        take_z1(tile)
                    if s == 1:
                        if c > 0:
                            take_gram(tile, c - 1, 0)
                        if c == 1 and later:
                            take_z2T(tile)
                    if s == 2 and c > 0:
                        take_gram(tile, c - 1, 1)
                    if s == 3 and c > 0:
                        take_gram(tile, c - 1, 3)

            for i in range(2):
                nc.vector.memset(e_diag[i][:, :, :, :, :].bitcast(F32), 0.0).then_inc(diag_zero, 1)
            dve.wait_ge(consts_in, 80)
            nc.vector.tensor_copy(sel_r[:, :], sel_sb).then_inc(sel_ready, 1)
            nc.vector.tensor_tensor(w0a_sb, w0a_sb, w0b_sb, ALU.add).then_inc(w0_sum, 1)
            dve.wait_ge(diag_zero, 2)
            for i in range(2):
                for g in range(NG):
                    last = nc.vector.tensor_copy(e_diag[i][:, g, 0, :, F], ones_sb[:, :])
                last.then_inc(diag_ready, 1)
            dve.wait_ge(w0_hi_done, 1)
            n = CHUNKS * H
            subtract(w0_lo[:, :, :].rearrange("p k h -> p (k h)"), w0a_sb[:, 0:n],
                     w0_hi[:, 0:CHUNKS, :].rearrange("p k h -> p (k h)").bitcast(F32))
            subtract(w0_hi[64:96, CHUNKS, :], w0a_sb[64:96, n:n + H],
                     w0_hi[64:96, CHUNKS, :].bitcast(F32)).then_inc(w0_ready, 1)
            for p in range(PARTS):
                dve.wait_ge(w1_hi_done, p + 1)
                subtract(w1_hl[:, p * PF:(p + 1) * PF, 1, :], w1_raw[:, :, :],
                         w1_hl[:, p * PF:(p + 1) * PF, 0, :].bitcast(F32)).then_inc(w1_lo_done, 1)
            do_tile(None)
            with dve.Fori(0, TILES - 1) as u:
                do_tile(u)
            end = TILES - 1
            take_x1T(end, -1)
            for g in range(NG):
                take_gram(end, -1, g)
            take_z1(end)
            sum_z2(end)
            take_z2T(end, True)


def kernel(**inputs):
    import concourse.bacc as bacc
    from concourse.bass_utils import run_bass_kernel_spmd

    partner, left = pair_tables()
    base = base_fields()

    sel = np.zeros((SPLIT, CHUNKS + 2, P), np.float32)
    rows = np.arange(P)
    left_rows = [(r + v, v, w) for r in (0, 32, 64) for v, w in left.items()]
    for s in range(2):
        sel[s * F + np.array(base), 0, rows] = 1
        for c in range(CHUNKS):
            sel[s * F + np.array(partner[c]), 1 + c, rows] = 1
        for p, _, w in left_rows:
            sel[s * F + w, 1 + CHUNKS, p] = 1

    w0 = np.asarray(inputs["L0_rec_W0"])
    w0a = np.zeros((P, CHUNKS + 1, H), w0.dtype)
    w0b = np.zeros((P, CHUNKS + 1, H), w0.dtype)
    for p, c, i, j in ([(p, c, base[p], partner[c][p]) for c in range(CHUNKS) for p in range(P)]
                       + [(p, CHUNKS, i, j) for p, i, j in left_rows]):
        w0a[p, c] = w0[:, i * F + j]
        if i != j:
            w0b[p, c] = w0[:, j * F + i]

    w1 = np.asarray(inputs["L0_rec_W1"]).reshape(H, H, F).transpose(1, 2, 0)
    arrays = {
        "ids": np.asarray(inputs["ids"]),
        "dense_t": np.asarray(inputs["dense_ctx"]).T,
        "sel": sel.reshape(SPLIT, -1),
        "ident": np.eye(P, dtype=np.float32),
        "ones_col": (np.arange(P)[:, None] // D == np.arange(GB)[None, :]).astype(np.float32),
        "w0a": w0a.reshape(P, -1),
        "w0b": w0b.reshape(P, -1),
        "w1": w1,
        "wt1": np.asarray(inputs["W_top1"]),
        "wt2": np.asarray(inputs["W_top2"]),
        "wt3": np.asarray(inputs["W_top3"]).reshape(M2 // P, P).T,
        "b1": np.asarray(inputs["b_top1"]).reshape(M1 // P, P).T,
        "b2": np.asarray(inputs["b_top2"]).reshape(M2 // P, P).T,
    }
    for f in range(F):
        arrays[f"tbl_{f}"] = np.asarray(inputs[f"tbl_{f}"])
    arrays = {n: np.ascontiguousarray(a) for n, a in arrays.items()}

    nc = bacc.Bacc("TRN2", target_bir_lowering=False, num_devices=1)
    aps = {n: nc.dram_tensor(f"{n}_dram", a.shape, mybir.dt.from_np(a.dtype), kind="ExternalInput").ap()
           for n, a in arrays.items()}
    out = nc.dram_tensor("y_dram", (1, B), F32, kind="ExternalOutput").ap()
    tables = [aps.pop(f"tbl_{f}") for f in range(F)]
    build(nc, tables=tables, out=out, **aps)
    r = run_bass_kernel_spmd(nc, [{f"{n}_dram": a for n, a in arrays.items()}], core_ids=[0])
    return r.results[0]["y_dram"].reshape(B, 1)
```

```python
from contextlib import ExitStack

import numpy as np

import concourse.bass as bass
from concourse import mybir

F32 = mybir.dt.float32
F32R = mybir.dt.float32r
I32 = mybir.dt.int32
ALU = mybir.AluOpType
ACT = mybir.ActivationFunctionType

P = 128
B, F, D, H = 512, 39, 16, 128
M1, M2, DENSE = 512, 256, 16
TILES = B // P
CB = 512 // D
COLS = P // CB
NG, GB = 4, 8
GF = F + 1
CHUNKS = 6
LEFT = F * (F + 1) // 2 - CHUNKS * P
STEPS = 4
SLOTS = COLS * STEPS
SPLIT = 2 * F
PARTS = 3
PF = F // PARTS
LAST = STEPS - 1
LROWS = 96


def base_fields():
    extra = list(range(LEFT, LEFT + P - 3 * F))
    return [p % 32 for p in range(96)] + [32 + (p % 7) for p in range(21)] + extra


def pair_tables():
    base = base_fields()
    want = [CHUNKS * base.count(v) + (v < LEFT) for v in range(F)]
    out = [{v} | {(v + s) % F for s in range(1, F // 2 + 1)} for v in range(F)]
    while True:
        over = [v for v in range(F) if len(out[v]) > want[v]]
        if not over:
            break
        came, queue = {over[0]: None}, [over[0]]
        for v in queue:
            if len(out[v]) < want[v]:
                break
            for w in sorted(out[v]):
                if w not in came:
                    came[w] = v
                    queue.append(w)
        while came[v] is not None:
            out[came[v]].remove(v)
            out[v].add(came[v])
            v = came[v]
    left = {v: sorted(out[v] - {v})[0] for v in range(LEFT)}
    rest = {v: sorted(out[v] - ({left[v]} if v in left else set())) for v in range(F)}
    partner = [[rest[base[p]].pop(0) for p in range(P)] for _ in range(CHUNKS)]
    return partner, left


def t_uses(first):
    uses = [("base", 0)] + ([] if first else [("xT", -1)])
    for c in range(COLS):
        if c > 0:
            uses.append(("xT", c - 1))
        if c + 1 < COLS:
            uses.append(("base", c + 1))
        if c == 1 and not first:
            uses.append(("zT", 0))
        uses.append(("tr", c))
    return uses


T_FIRST, T_LATER, T_END = t_uses(True), t_uses(False), [("xT", -1), ("zT", 0)]


def count(tile, per_tile, k):
    return k if tile is None else tile * per_tile + (per_tile + k)


def t_count(tile, use, end=False):
    if tile is None:
        return T_FIRST.index(use) + 1
    return tile * len(T_LATER) + (len(T_FIRST) + (T_END if end else T_LATER).index(use) + 1)


def build(nc, ids, dense_t, sel, ident, ones_col, w0a, w0b, w1, wt1, wt2, wt3, b1, b2, tables, out):
    ctx = ExitStack()
    with ctx:
        def sb(name, shape, dt=F32):
            return ctx.enter_context(nc.sbuf_tensor(name, shape, dt))

        def ps(name, shape):
            return ctx.enter_context(nc.psum_tensor(name, shape, F32))

        def sem(name):
            return ctx.enter_context(nc.semaphore(name))

        ids_sb = sb("ids_sb", [P, TILES * F], I32)
        idx = sb("idx", [P, F], I32)
        emb = sb("emb", [P, F * D])
        emb_split = sb("emb_split", [P, SPLIT, D])
        embT = sb("embT", [SPLIT, P, D], F32R)
        sel_r = sb("sel_r", [SPLIT, (CHUNKS + 2) * P], F32R)
        ident_sb = sb("ident_sb", [P, P])
        base_sb = sb("base_sb", [P, 2, 512])
        prod = sb("prod", [P, STEPS, 2, 512])
        prod_hi = sb("prod_hi", [P, STEPS, 2, 512], F32R)
        prod_lo = sb("prod_lo", [P, LAST, 2, 512], F32R)
        w0_hi = sb("w0_hi", [P, CHUNKS + 1, H], F32R)
        w0_lo = sb("w0_lo", [P, CHUNKS, H], F32R)
        w1_hl = sb("w1_hl", [P, F, 2, H], F32R)
        w1_raw = sb("w1_raw", [P, PF, H])
        x1_sb = sb("x1_sb", [P, 512])
        x1T_hi = sb("x1T_hi", [P, NG, H], F32R)
        x1T_lo = sb("x1T_lo", [P, NG, H], F32R)
        e_rows = sb("e_rows", [P, NG, SPLIT])
        e_diag = [sb(f"e_diag{i}", [P, NG, 2, GB, GF], F32R) for i in range(2)]
        ones_sb = sb("ones_sb", [P, GB])
        gram_hi = sb("gram_hi", [P, GF, P], F32R)
        gram_lo = sb("gram_lo", [P, GF, P], F32R)
        z2_part = sb("z2_part", [P, H])
        z2_rows = sb("z2_rows", [P, H])
        z1T = sb("z1T", [P, B])
        z2T = sb("z2T", [P, B])
        denseT = sb("denseT", [DENSE, B])
        wt1_sb = sb("wt1_sb", [P, 2, M1])
        wt1d_sb = sb("wt1d_sb", [DENSE, M1])
        wt2_sb = sb("wt2_sb", [P, M1 // P, M2])
        wt3_sb = sb("wt3_sb", [P, M2 // P])
        b1_sb = sb("b1_sb", [P, M1 // P])
        b2_sb = sb("b2_sb", [P, M2 // P])
        y_sb = sb("y_sb", [1, B])
        w0a_sb = prod[:, 0, :, :].rearrange("p a n -> p (a n)")[:, 0:(CHUNKS + 1) * H]
        w0b_sb = prod[:, 1, :, :].rearrange("p a n -> p (a n)")[:, 0:(CHUNKS + 1) * H]
        sel_sb = prod[0:SPLIT, 2, :, :].rearrange("p a n -> p (a n)")
        h1 = prod[:, 0:2, :, :].rearrange("p s a n -> p (s a) n")
        h2 = prod[:, 2, :, :]

        sel_ps = [ps(f"sel_ps{i}", [P, 2, 512]) for i in range(2)]
        x1_ps = ps("x1_ps", [P, 512])
        t_ps = ps("t_ps", [P, 512])
        gz_ps = [ps(f"gz_ps{i}", [P, 512]) for i in range(2)]
        z_ps = gz_ps[1]

        ids_in = sem("ids_in")
        consts_in = sem("consts_in")
        w1_in = sem("w1_in")
        tower_in = sem("tower_in")
        idx_ready = sem("idx_ready")
        look_up_begun = sem("look_up_begun")
        looked_up = [sem(f"looked_up{p}") for p in range(PARTS)]
        sel_ready = sem("sel_ready")
        w0_sum = sem("w0_sum")
        w0_hi_done = sem("w0_hi_done")
        w0_ready = sem("w0_ready")
        w1_hi_done = sem("w1_hi_done")
        w1_lo_done = sem("w1_lo_done")
        diag_zero = sem("diag_zero")
        diag_ready = sem("diag_ready")
        emb_hi_done = sem("emb_hi_done")
        emb_lo_done = sem("emb_lo_done")
        emb_turned = sem("emb_turned")
        embT_done = sem("embT_done")
        t_full = sem("t_full")
        xT_hi_done = sem("xT_hi_done")
        t_free = sem("t_free")
        sel_done = sem("sel_done")
        mult_done = sem("mult_done")
        hi_done = sem("hi_done")
        lo_done = sem("lo_done")
        main_done = sem("main_done")
        x1_taken = sem("x1_taken")
        diag_in = [sem(f"diag_in{i}") for i in range(2)]
        g_done = sem("g_done")
        g_hi_done = sem("g_hi_done")
        g_taken = sem("g_taken")
        z_done = sem("z_done")
        z_part_done = sem("z_part_done")
        z_sum_done = sem("z_sum_done")
        z1_done = sem("z1_done")
        h1_ps_done = sem("h1_ps_done")
        h1_done = sem("h1_done")
        h2_ps_done = sem("h2_ps_done")
        h2_done = sem("h2_done")
        y_ps_done = sem("y_ps_done")
        y_done = sem("y_done")
        y_out = sem("y_out")

        block = ctx.enter_context(nc.Block())

        @block.sync
        def _(sp):
            sp.dma_start(ids_sb[:, :].rearrange("p (t f) -> p t f", f=F),
                         ids.rearrange("(t p) f -> p t f", p=P)).then_inc(ids_in, 16)
            sp.dma_start(sel_sb, sel).then_inc(consts_in, 16)
            sp.dma_start(w0a_sb, w0a).then_inc(consts_in, 16)
            sp.dma_start(w0b_sb, w0b).then_inc(consts_in, 16)
            sp.dma_start(ident_sb[:, :], ident).then_inc(consts_in, 16)
            sp.dma_start(ones_sb[:, :], ones_col).then_inc(consts_in, 16)
            for p in range(PARTS):
                if p > 0:
                    sp.wait_ge(w1_lo_done, p)
                sp.dma_start(w1_raw[:, :, :], w1[:, p * PF:(p + 1) * PF, :]).then_inc(w1_in, 16)
            sp.dma_start(denseT[:, :], dense_t).then_inc(tower_in, 16)
            sp.dma_start(wt1_sb[:, :, :], wt1[0:2 * P, :].rearrange("(k p) n -> p k n", p=P)).then_inc(tower_in, 16)
            sp.dma_start(wt1d_sb[:, :], wt1[2 * P:2 * P + DENSE, :]).then_inc(tower_in, 16)
            sp.dma_start(wt2_sb[:, :, :], wt2.rearrange("(k p) n -> p k n", p=P)).then_inc(tower_in, 16)
            sp.dma_start(wt3_sb[:, :], wt3).then_inc(tower_in, 16)
            sp.dma_start(b1_sb[:, :], b1).then_inc(tower_in, 16)
            sp.dma_start(b2_sb[:, :], b2).then_inc(tower_in, 16)
            sp.wait_ge(diag_ready, 2)

            def diagonals(tile):
                for c in range(COLS):
                    sp.wait_ge(t_free, t_count(tile, ("tr", c)))
                    for g in range(GB):
                        rows = slice(g * D, (g + 1) * D)
                        sp.dma_start(e_diag[c % 2][rows, :, :, g, 0:F].bitcast(F32),
                                     e_rows[rows, :, :].rearrange("p n (s f) -> p n s f", s=2),
                                     ).then_inc(diag_in[c % 2], 16)

            diagonals(None)
            with sp.Fori(0, TILES - 1) as u:
                diagonals(u)
            sp.wait_ge(y_done, 1)
            sp.dma_start(out, y_sb[:, :]).then_inc(y_out, 16)
            sp.wait_ge(y_out, 16)

        @block.gpsimd
        def _(pool):
            pool.wait_ge(ids_in, 16)

            def look_up(tile):
                first = 0 if tile is None else (tile + 1) * F
                for p in range(PARTS):
                    if tile is not None:
                        pool.wait_ge(emb_lo_done, tile * PARTS + (p + 1))
                    nc.gpsimd.tensor_copy(idx[:, p * PF:(p + 1) * PF],
                                          ids_sb[:, bass.ds(first + p * PF, PF)]).then_inc(idx_ready, 1)
                    pool.wait_ge(idx_ready, count(tile, PARTS, p + 1))
                    pool.sem_inc(look_up_begun, 1)
                    for f in range(p * PF, (p + 1) * PF):
                        pool.indirect_dma_start(
                            emb[:, f * D:(f + 1) * D], None, tables[f],
                            bass.IndirectOffsetOnAxis(ap=idx[:, f:f + 1], axis=0),
                        ).then_inc(looked_up[p], 16)

            look_up(None)
            with pool.Fori(0, TILES - 1) as u:
                look_up(u)

        @block.tensor
        def _(pe):
            def selector(c):
                return sel_r[:, c * P:(c + 1) * P]

            def column(c):
                return embT[:, c * CB:(c + 1) * CB, :].rearrange("p b d -> p (b d)")

            def t_turn(tile, use, end=False):
                if tile is not None or use != T_FIRST[0]:
                    pe.wait_ge(t_free, count_before(tile, use, end))

            def count_before(tile, use, end):
                if tile is None:
                    return T_FIRST.index(use)
                return tile * len(T_LATER) + (len(T_FIRST) + (T_END if end else T_LATER).index(use))

            def transpose_emb(tile, q):
                if q == 0:
                    pe.wait_ge(emb_lo_done, count(tile, PARTS, PARTS))
                if tile is not None:
                    pe.wait_ge(mult_done, count(tile, SLOTS, q - 1))
                for k in range(8):
                    mm = nc.tensor.transpose(sel_ps[q][0:SPLIT, k // 4, (k % 4) * P:(k % 4 + 1) * P],
                                             emb_split[:, :, 8 * q + k], ident_sb[:, :])
                mm.then_inc(emb_turned, 1)

            def base_rows(tile, c):
                t_turn(tile, ("base", c))
                nc.tensor.matmul(t_ps[:, :], selector(0), column(c), start=True, stop=True).then_inc(t_full, 1)

            def emb_rows(tile, c):
                t_turn(tile, ("tr", c))
                for g in range(NG):
                    b0 = c * CB + g * GB
                    mm = nc.tensor.transpose(
                        t_ps[:, g * SPLIT:(g + 1) * SPLIT],
                        embT[:, b0:b0 + GB, :].rearrange("p b d -> p (b d)").bitcast(F32),
                        ident_sb[0:SPLIT, 0:SPLIT])
                mm.then_inc(t_full, 1)

            def transpose_x1(tile, c, end=False):
                t_turn(tile, ("xT", c), end)
                pe.wait_ge(x1_taken, count(tile, COLS, c + 1))
                for g in range(NG):
                    mm = nc.tensor.transpose(t_ps[:, g * P:(g + 1) * P], x1_sb[:, g * P:(g + 1) * P],
                                             ident_sb[:, :])
                mm.then_inc(t_full, 1)

            def partners(tile, n):
                c, s = divmod(n, STEPS)
                if n >= 2:
                    pe.wait_ge(mult_done, count(tile, SLOTS, n - 1))
                if n == 0:
                    pe.wait_ge(embT_done, count(tile, 2, 2))
                    if tile is None:
                        pe.wait_ge(sel_ready, 1)
                if s < LAST:
                    for a in range(2):
                        mm = nc.tensor.matmul(sel_ps[s % 2][:, a, :], selector(1 + 2 * s + a), column(c),
                                              start=True, stop=True)
                else:
                    mm = nc.tensor.matmul(sel_ps[s % 2][0:LROWS, 0, :], selector(1 + CHUNKS)[:, 0:LROWS],
                                          column(c), start=True, stop=True)
                mm.then_inc(sel_done, 1)

            def main(tile, n):
                c, s = divmod(n, STEPS)
                if tile is None and n == 0:
                    pe.wait_ge(w0_ready, 1)
                if s == 0 and (tile is not None or c > 0):
                    pe.wait_ge(x1_taken, count(tile, COLS, c))
                pe.wait_ge(lo_done, count(tile, SLOTS, n + 1))
                if s < LAST:
                    for a in range(2):
                        k = 2 * s + a
                        hi, lo = prod_hi[:, s, a, :], prod_lo[:, s, a, :]
                        nc.tensor.matmul(x1_ps[:, :], w0_hi[:, k, :], hi, start=(k == 0), stop=False)
                        nc.tensor.matmul(x1_ps[:, :], w0_hi[:, k, :], lo, start=False, stop=False)
                        mm = nc.tensor.matmul(x1_ps[:, :], w0_lo[:, k, :], hi, start=False, stop=False)
                else:
                    mm = nc.tensor.matmul(x1_ps[:, :], w0_hi[0:LROWS, CHUNKS, :], prod_hi[0:LROWS, s, 0, :],
                                          start=False, stop=True)
                mm.then_inc(main_done, 1)

            def gram(tile, c, g, end=False):
                if g == 0:
                    if c == -2:
                        pe.wait_ge(t_free, t_count_of_column_2(tile))
                    else:
                        pe.wait_ge(t_free, t_count(tile, ("xT", c), end))
                    if c < 0:
                        pe.wait_ge(diag_in[c % 2], tile * (2 * 16 * GB) + 2 * 16 * GB)
                    else:
                        pe.wait_ge(diag_in[c % 2], count(tile, 2 * 16 * GB, 16 * GB * (c // 2 + 1)))
                if tile is not None or c > 0 or g > 1:
                    pe.wait_ge(g_taken, count(tile, SLOTS, NG * c + g - 1))
                if tile is not None and (c, g) == (0, 1):
                    pe.wait_ge(z_sum_done, tile + 1)
                o = gz_ps[g % 2][:, 0:GB * GF]
                e_hi = e_diag[c % 2][:, g, 0, :, :].rearrange("p b f -> p (b f)")
                e_lo = e_diag[c % 2][:, g, 1, :, :].rearrange("p b f -> p (b f)")
                nc.tensor.matmul(o, x1T_hi[:, g, :], e_hi, start=True, stop=False)
                nc.tensor.matmul(o, x1T_hi[:, g, :], e_lo, start=False, stop=False)
                nc.tensor.matmul(o, x1T_lo[:, g, :], e_hi, start=False, stop=True).then_inc(g_done, 1)

            def layer2(tile, j0, j1):
                if j0 == 0:
                    pe.wait_ge(g_taken, count(tile, SLOTS, 0))
                for j in range(j0, j1):
                    w = w1_hl[:, j, :, :].rearrange("p s h -> p (s h)")
                    nc.tensor.matmul(z_ps[:, 0:2 * H], gram_hi[:, j, :], w, start=(j == 0), stop=False)
                    mm = nc.tensor.matmul(z_ps[:, 0:2 * H], gram_lo[:, j, :], w, start=False,
                                          stop=(j == F - 1))
                if j1 == F:
                    mm.then_inc(z_done, 1)

            def t_count_of_column_2(tile):
                return tile * len(T_LATER) + (T_FIRST.index(("xT", 2)) + 1)

            def transpose_z2(tile, end=False):
                t_turn(tile, ("zT", 0), end)
                pe.wait_ge(z_sum_done, tile + 1)
                nc.tensor.transpose(t_ps[:, 0:P], z2_rows[:, :], ident_sb[:, :]).then_inc(t_full, 1)

            def do_tile(tile):
                later = tile is not None
                transpose_emb(tile, 0)
                if later:
                    gram(tile, -2, 0)
                transpose_emb(tile, 1)
                if later:
                    gram(tile, -2, 1)
                    main(tile, -2)
                    gram(tile, -2, 2)
                    main(tile, -1)
                partners(tile, 0)
                base_rows(tile, 0)
                if later:
                    gram(tile, -2, 3)
                partners(tile, 1)
                if later:
                    transpose_x1(tile, -1)
                for n in range(SLOTS - 2):
                    c, s = divmod(n, STEPS)
                    partners(tile, n + 2)
                    main(tile, n)
                    if c == 0 and later:
                        if s < 2:
                            if s == 1:
                                base_rows(tile, 1)
                            gram(tile, -1, 2 * s)
                            gram(tile, -1, 2 * s + 1)
                        if s == 2:
                            emb_rows(tile, 0)
                            layer2(tile, 0, F // 3)
                        if s == 3:
                            layer2(tile, F // 3, 2 * F // 3)
                        continue
                    if s == 0 and c > 0:
                        transpose_x1(tile, c - 1)
                        if c == 1 and later:
                            layer2(tile, 2 * F // 3, F)
                    if s == 1:
                        if c + 1 < COLS:
                            base_rows(tile, c + 1)
                        else:
                            emb_rows(tile, c)
                        if c == 1 and later:
                            transpose_z2(tile)
                    if s == 2:
                        if c > 0:
                            gram(tile, c - 1, 0)
                            gram(tile, c - 1, 1)
                        emb_rows(tile, c)
                    if s == 3 and c > 0:
                        gram(tile, c - 1, 2)
                        gram(tile, c - 1, 3)

            pe.wait_ge(consts_in, 80)
            do_tile(None)
            pe.wait_ge(w1_lo_done, PARTS)
            with pe.Fori(0, TILES - 1) as u:
                do_tile(u)
            end = TILES - 1
            for g in range(NG):
                gram(end, -2, g, True)
                if g in (1, 2):
                    main(end, g - 3)
            transpose_x1(end, -1, True)
            for g in range(NG):
                gram(end, -1, g, True)
            layer2(end, 0, F)
            transpose_z2(end, True)

            pe.wait_ge(tower_in, 7 * 16)
            pe.wait_ge(t_free, t_count(end, ("zT", 0), True))
            for m in range(M1 // P):
                o = sel_ps[m // 2][:, m % 2, :]
                cols = slice(m * P, (m + 1) * P)
                nc.tensor.matmul(o, wt1_sb[:, 0, cols], z1T[:, :], start=True, stop=False)
                nc.tensor.matmul(o, wt1_sb[:, 1, cols], z2T[:, :], start=False, stop=False)
                nc.tensor.matmul(o, wt1d_sb[:, cols], denseT[:, :], start=False, stop=True).then_inc(h1_ps_done, 1)
            for m in range(M2 // P):
                o = [x1_ps, gz_ps[0]][m]
                for k in range(M1 // P):
                    pe.wait_ge(h1_done, k + 1)
                    mm = nc.tensor.matmul(o[:, :], wt2_sb[:, k, m * P:(m + 1) * P], h1[:, k, :],
                                          start=(k == 0), stop=(k == M1 // P - 1))
                mm.then_inc(h2_ps_done, 1)
            for k in range(M2 // P):
                pe.wait_ge(h2_done, k + 1)
                mm = nc.tensor.matmul(t_ps[0:1, :], wt3_sb[:, k:k + 1], h2[:, k, :],
                                      start=(k == 0), stop=(k == M2 // P - 1))
            mm.then_inc(y_ps_done, 1)

        @block.scalar
        def _(act):
            def copy(o, i):
                return nc.scalar.activation(o, i, ACT.Copy)

            def split_emb(tile):
                for p in range(PARTS):
                    act.wait_ge(looked_up[p], count(tile, 16 * PF, 16 * PF))
                    fields = slice(p * PF, (p + 1) * PF)
                    copy(emb_split[:, fields, :].bitcast(F32R),
                         emb[:, p * PF * D:(p + 1) * PF * D].rearrange("p (f d) -> p f d", d=D),
                         ).then_inc(emb_hi_done, 1)

            def take_embT(tile, q):
                act.wait_ge(emb_turned, count(tile, 2, q + 1))
                copy(embT[:, :, 8 * q:8 * q + 8].rearrange("p b d -> p d b"),
                     sel_ps[q][0:SPLIT, :, :].rearrange("p a (d b) -> p (a d) b", d=4)).then_inc(embT_done, 1)

            def take_base(tile, c):
                act.wait_ge(t_full, t_count(tile, ("base", c)))
                if tile is not None or c >= 2:
                    act.wait_ge(mult_done, count(tile, SLOTS, STEPS * (c - 1)))
                copy(base_sb[:, c % 2, :], t_ps[:, :]).then_inc(t_free, 1)

            def take_emb_rows(tile, c):
                act.wait_ge(t_full, t_count(tile, ("tr", c)))
                if tile is not None or c > 0:
                    if c % 2:
                        act.wait_ge(diag_in[0], count(tile, 2 * 16 * GB, 16 * GB * (c // 2 + 1)))
                    else:
                        act.wait_ge(diag_in[1], count(tile, 2 * 16 * GB, 16 * GB * (c // 2)))
                copy(e_rows[:, :, :].rearrange("p n f -> p (n f)"), t_ps[:, 0:NG * SPLIT]).then_inc(t_free, 1)

            def take_x1T(tile, c, end=False):
                act.wait_ge(t_full, t_count(tile, ("xT", c), end))
                copy(x1T_hi[:, :, :].rearrange("p n h -> p (n h)"), t_ps[:, :]).then_inc(xT_hi_done, 1)

            def products_hi(tile, n):
                s = n % STEPS
                act.wait_ge(mult_done, count(tile, SLOTS, n + 1))
                if tile is not None or n >= STEPS:
                    act.wait_ge(main_done, count(tile, SLOTS, n - STEPS + 1))
                if s < LAST:
                    copy(prod_hi[:, s, :, :], prod[:, s, :, :]).then_inc(hi_done, 1)
                else:
                    copy(prod_hi[0:LROWS, s, 0, :], prod[0:LROWS, s, 0, :]).then_inc(hi_done, 1)

            def take_x1(tile, c):
                act.wait_ge(main_done, count(tile, SLOTS, STEPS * (c + 1)))
                copy(x1_sb[:, :], x1_ps[:, :]).then_inc(x1_taken, 1)

            def take_gram(tile, c, g):
                act.wait_ge(g_done, count(tile, SLOTS, NG * c + g + 1))
                if tile is not None and c == 0 and g == 0:
                    act.wait_ge(z_done, tile + 1)
                    act.wait_ge(z1_done, tile + 1)
                b0 = (c % COLS) * CB + g * GB
                copy(gram_hi[:, :, b0:b0 + GB].rearrange("p j b -> p b j"),
                     gz_ps[g % 2][:, 0:GB * GF].rearrange("p (b j) -> p b j", b=GB)).then_inc(g_hi_done, 1)

            def take_z2(tile):
                act.wait_ge(z_done, tile + 1)
                copy(z2_part[:, :], z_ps[:, H:2 * H]).then_inc(z_part_done, 1)

            def do_tile(tile):
                later = tile is not None
                split_emb(tile)
                if later:
                    products_hi(tile, -1)
                take_embT(tile, 0)
                if later:
                    take_gram(tile, -2, 0)
                take_embT(tile, 1)
                if later:
                    take_gram(tile, -2, 1)
                    take_gram(tile, -2, 2)
                take_base(tile, 0)
                if later:
                    take_x1(tile, -1)
                    take_gram(tile, -2, 3)
                products_hi(tile, 0)
                if later:
                    take_x1T(tile, -1)
                for n in range(SLOTS - 2):
                    c, s = divmod(n, STEPS)
                    products_hi(tile, n + 1)
                    if c == 0 and later and s < 2:
                        if s == 1:
                            take_base(tile, 1)
                        take_gram(tile, -1, 2 * s)
                        take_gram(tile, -1, 2 * s + 1)
                        continue
                    if s == 0 and c > 0:
                        take_x1T(tile, c - 1)
                        if c == 1 and later:
                            take_z2(tile)
                    if s == 1:
                        if c + 1 < COLS:
                            take_base(tile, c + 1)
                        else:
                            take_emb_rows(tile, c)
                    if s == 2:
                        if c > 0:
                            take_gram(tile, c - 1, 0)
                            take_gram(tile, c - 1, 1)
                        take_emb_rows(tile, c)
                    if s == 3:
                        take_x1(tile, c)
                        if c > 0:
                            take_gram(tile, c - 1, 2)
                            take_gram(tile, c - 1, 3)

            act.wait_ge(w0_sum, 1)
            copy(w0_hi[:, :, :].rearrange("p k h -> p (k h)"), w0a_sb).then_inc(w0_hi_done, 1)
            for p in range(PARTS):
                act.wait_ge(w1_in, 16 * (p + 1))
                copy(w1_hl[:, p * PF:(p + 1) * PF, 0, :], w1_raw[:, :, :]).then_inc(w1_hi_done, 1)
            do_tile(None)
            with act.Fori(0, TILES - 1) as u:
                do_tile(u)
            end = TILES - 1
            products_hi(end, -1)
            for g in range(NG):
                take_gram(end, -2, g)
            take_x1(end, -1)
            take_x1T(end, -1, True)
            for g in range(NG):
                take_gram(end, -1, g)
            take_z2(end)

            act.wait_ge(tower_in, 7 * 16)
            for m in range(M1 // P):
                act.wait_ge(h1_ps_done, m + 1)
                nc.scalar.activation(h1[:, m, :], sel_ps[m // 2][:, m % 2, :], ACT.Relu,
                                     bias=b1_sb[:, m:m + 1]).then_inc(h1_done, 1)
            for m in range(M2 // P):
                act.wait_ge(h2_ps_done, m + 1)
                nc.scalar.activation(h2[:, m, :], [x1_ps, gz_ps[0]][m][:, :], ACT.Relu,
                                     bias=b2_sb[:, m:m + 1]).then_inc(h2_done, 1)
            act.wait_ge(y_ps_done, 1)
            copy(y_sb[:, :], t_ps[0:1, :]).then_inc(y_done, 1)

        @block.vector
        def _(dve):
            def subtract(o, whole, hi):
                return nc.vector.tensor_tensor(o, whole, hi, ALU.subtract)

            def split_emb(tile):
                for p in range(PARTS):
                    dve.wait_ge(emb_hi_done, count(tile, PARTS, p + 1))
                    subtract(emb_split[:, F + p * PF:F + (p + 1) * PF, :],
                             emb[:, p * PF * D:(p + 1) * PF * D].rearrange("p (f d) -> p f d", d=D),
                             emb_split[:, p * PF:(p + 1) * PF, :]).then_inc(emb_lo_done, 1)

            def multiply(tile, n):
                c, s = divmod(n, STEPS)
                dve.wait_ge(sel_done, count(tile, SLOTS, n + 1))
                if s == 0:
                    dve.wait_ge(t_free, t_count(tile, ("base", c)))
                if tile is not None or n >= STEPS:
                    dve.wait_ge(hi_done, count(tile, SLOTS, n - STEPS + 1))
                if s < LAST:
                    base = base_sb[:, c % 2, :].unsqueeze(1).to_broadcast([P, 2, 512])
                    nc.vector.tensor_tensor(prod[:, s, :, :], sel_ps[s % 2][:, :, :], base,
                                            ALU.mult).then_inc(mult_done, 1)
                else:
                    nc.vector.tensor_tensor(prod[0:LROWS, s, 0, :], sel_ps[s % 2][0:LROWS, 0, :],
                                            base_sb[0:LROWS, c % 2, :], ALU.mult).then_inc(mult_done, 1)

            def products_lo(tile, n):
                s = n % STEPS
                dve.wait_ge(hi_done, count(tile, SLOTS, n + 1))
                if tile is not None or n >= STEPS:
                    dve.wait_ge(main_done, count(tile, SLOTS, n - STEPS + 1))
                if s < LAST:
                    subtract(prod_lo[:, s, :, :], prod[:, s, :, :],
                             prod_hi[:, s, :, :].bitcast(F32)).then_inc(lo_done, 1)
                else:
                    subtract(prod_hi[32:64, s, 0, :], prod[32:64, s, 0, :],
                             prod_hi[32:64, s, 0, :].bitcast(F32)).then_inc(lo_done, 1)

            def take_x1T(tile, c):
                dve.wait_ge(xT_hi_done, count(tile, COLS, c + 1))
                subtract(x1T_lo[:, :, :].rearrange("p n h -> p (n h)"), t_ps[:, :],
                         x1T_hi[:, :, :].rearrange("p n h -> p (n h)").bitcast(F32)).then_inc(t_free, 1)

            def take_gram(tile, c, g):
                dve.wait_ge(g_hi_done, count(tile, SLOTS, NG * c + g + 1))
                b0 = (c % COLS) * CB + g * GB
                subtract(gram_lo[:, :, b0:b0 + GB].rearrange("p j b -> p b j"),
                         gz_ps[g % 2][:, 0:GB * GF].rearrange("p (b j) -> p b j", b=GB),
                         gram_hi[:, :, b0:b0 + GB].rearrange("p j b -> p b j").bitcast(F32),
                         ).then_inc(g_taken, 1)

            def sum_z2(tile):
                dve.wait_ge(z_part_done, tile + 1)
                nc.vector.tensor_tensor(z2_rows[:, :], z_ps[:, 0:H], z2_part[:, :],
                                        ALU.add).then_inc(z_sum_done, 1)

            def take_z1(tile):
                dve.wait_ge(g_taken, count(tile, SLOTS, 0))
                nc.vector.tensor_tensor(z1T[:, bass.ds(tile * P, P)], gram_hi[:, F, :].bitcast(F32),
                                        gram_lo[:, F, :].bitcast(F32), ALU.add).then_inc(z1_done, 1)

            def take_z2T(tile, end=False):
                dve.wait_ge(t_full, t_count(tile, ("zT", 0), end))
                nc.vector.tensor_copy(z2T[:, bass.ds(tile * P, P)], t_ps[:, 0:P]).then_inc(t_free, 1)

            def do_tile(tile):
                later = tile is not None
                split_emb(tile)
                if later:
                    products_lo(tile, -1)
                    take_gram(tile, -2, 0)
                    take_gram(tile, -2, 1)
                    take_gram(tile, -2, 2)
                multiply(tile, 0)
                multiply(tile, 1)
                if later:
                    take_gram(tile, -2, 3)
                products_lo(tile, 0)
                if later:
                    take_x1T(tile, -1)
                for n in range(SLOTS - 2):
                    c, s = divmod(n, STEPS)
                    multiply(tile, n + 2)
                    products_lo(tile, n + 1)
                    if c == 0 and later and s < 2:
                        take_gram(tile, -1, 2 * s)
                        take_gram(tile, -1, 2 * s + 1)
                    if s == 0 and c > 0:
                        take_x1T(tile, c - 1)
                        if c == 1 and later:
                            sum_z2(tile)
                            take_z1(tile)
                    if s == 1 and c == 1 and later:
                        take_z2T(tile)
                    if s == 2 and c > 0:
                        take_gram(tile, c - 1, 0)
                        take_gram(tile, c - 1, 1)
                    if s == 3 and c > 0:
                        take_gram(tile, c - 1, 2)
                        take_gram(tile, c - 1, 3)

            for i in range(2):
                nc.vector.memset(e_diag[i][:, :, :, :, :].bitcast(F32), 0.0).then_inc(diag_zero, 1)
            dve.wait_ge(consts_in, 80)
            nc.vector.tensor_copy(sel_r[:, :], sel_sb).then_inc(sel_ready, 1)
            nc.vector.tensor_tensor(w0a_sb, w0a_sb, w0b_sb, ALU.add).then_inc(w0_sum, 1)
            dve.wait_ge(diag_zero, 2)
            for i in range(2):
                for g in range(NG):
                    last = nc.vector.tensor_copy(e_diag[i][:, g, 0, :, F], ones_sb[:, :])
                last.then_inc(diag_ready, 1)
            dve.wait_ge(w0_hi_done, 1)
            n = CHUNKS * H
            subtract(w0_lo[:, :, :].rearrange("p k h -> p (k h)"), w0a_sb[:, 0:n],
                     w0_hi[:, 0:CHUNKS, :].rearrange("p k h -> p (k h)").bitcast(F32))
            subtract(w0_hi[64:96, CHUNKS, :], w0a_sb[64:96, n:n + H],
                     w0_hi[64:96, CHUNKS, :].bitcast(F32)).then_inc(w0_ready, 1)
            for p in range(PARTS):
                dve.wait_ge(w1_hi_done, p + 1)
                subtract(w1_hl[:, p * PF:(p + 1) * PF, 1, :], w1_raw[:, :, :],
                         w1_hl[:, p * PF:(p + 1) * PF, 0, :].bitcast(F32)).then_inc(w1_lo_done, 1)
            do_tile(None)
            with dve.Fori(0, TILES - 1) as u:
                do_tile(u)
            end = TILES - 1
            products_lo(end, -1)
            for g in range(NG):
                take_gram(end, -2, g)
            take_x1T(end, -1)
            for g in range(NG):
                take_gram(end, -1, g)
            take_z1(end)
            sum_z2(end)
            take_z2T(end, True)


def kernel(**inputs):
    import concourse.bacc as bacc
    from concourse.bass_utils import run_bass_kernel_spmd

    partner, left = pair_tables()
    base = base_fields()

    sel = np.zeros((SPLIT, CHUNKS + 2, P), np.float32)
    rows = np.arange(P)
    left_rows = [(r + v, v, w) for r in (0, 32, 64) for v, w in left.items()]
    for s in range(2):
        sel[s * F + np.array(base), 0, rows] = 1
        for c in range(CHUNKS):
            sel[s * F + np.array(partner[c]), 1 + c, rows] = 1
        for p, _, w in left_rows:
            sel[s * F + w, 1 + CHUNKS, p] = 1

    w0 = np.asarray(inputs["L0_rec_W0"])
    w0a = np.zeros((P, CHUNKS + 1, H), w0.dtype)
    w0b = np.zeros((P, CHUNKS + 1, H), w0.dtype)
    for p, c, i, j in ([(p, c, base[p], partner[c][p]) for c in range(CHUNKS) for p in range(P)]
                       + [(p, CHUNKS, i, j) for p, i, j in left_rows]):
        w0a[p, c] = w0[:, i * F + j]
        if i != j:
            w0b[p, c] = w0[:, j * F + i]

    w1 = np.asarray(inputs["L0_rec_W1"]).reshape(H, H, F).transpose(1, 2, 0)
    arrays = {
        "ids": np.asarray(inputs["ids"]),
        "dense_t": np.asarray(inputs["dense_ctx"]).T,
        "sel": sel.reshape(SPLIT, -1),
        "ident": np.eye(P, dtype=np.float32),
        "ones_col": (np.arange(P)[:, None] // D == np.arange(GB)[None, :]).astype(np.float32),
        "w0a": w0a.reshape(P, -1),
        "w0b": w0b.reshape(P, -1),
        "w1": w1,
        "wt1": np.asarray(inputs["W_top1"]),
        "wt2": np.asarray(inputs["W_top2"]),
        "wt3": np.asarray(inputs["W_top3"]).reshape(M2 // P, P).T,
        "b1": np.asarray(inputs["b_top1"]).reshape(M1 // P, P).T,
        "b2": np.asarray(inputs["b_top2"]).reshape(M2 // P, P).T,
    }
    for f in range(F):
        arrays[f"tbl_{f}"] = np.asarray(inputs[f"tbl_{f}"])
    arrays = {n: np.ascontiguousarray(a) for n, a in arrays.items()}

    nc = bacc.Bacc("TRN2", target_bir_lowering=False, num_devices=1)
    aps = {n: nc.dram_tensor(f"{n}_dram", a.shape, mybir.dt.from_np(a.dtype), kind="ExternalInput").ap()
           for n, a in arrays.items()}
    out = nc.dram_tensor("y_dram", (1, B), F32, kind="ExternalOutput").ap()
    tables = [aps.pop(f"tbl_{f}") for f in range(F)]
    build(nc, tables=tables, out=out, **aps)
    r = run_bass_kernel_spmd(nc, [{f"{n}_dram": a for n, a in arrays.items()}], core_ids=[0])
    return r.results[0]["y_dram"].reshape(B, 1)
```

```python
from contextlib import ExitStack

import numpy as np

import concourse.bass as bass
from concourse import mybir

F32 = mybir.dt.float32
F32R = mybir.dt.float32r
I32 = mybir.dt.int32
ALU = mybir.AluOpType
ACT = mybir.ActivationFunctionType

P = 128
B, F, D, H = 512, 39, 16, 128
M1, M2, DENSE = 512, 256, 16
TILES = B // P
CB = 512 // D
COLS = P // CB
NG, GB = 4, 8
GF = F + 1
CHUNKS = 6
LEFT = F * (F + 1) // 2 - CHUNKS * P
STEPS = 4
SLOTS = COLS * STEPS
SPLIT = 2 * F
PARTS = 3
PF = F // PARTS
LAST = STEPS - 1
E = B - P
LROWS = 96


def base_fields():
    extra = list(range(LEFT, LEFT + P - 3 * F))
    return [p % 32 for p in range(96)] + [32 + (p % 7) for p in range(21)] + extra


def pair_tables():
    base = base_fields()
    want = [CHUNKS * base.count(v) + (v < LEFT) for v in range(F)]
    out = [{v} | {(v + s) % F for s in range(1, F // 2 + 1)} for v in range(F)]
    while True:
        over = [v for v in range(F) if len(out[v]) > want[v]]
        if not over:
            break
        came, queue = {over[0]: None}, [over[0]]
        for v in queue:
            if len(out[v]) < want[v]:
                break
            for w in sorted(out[v]):
                if w not in came:
                    came[w] = v
                    queue.append(w)
        while came[v] is not None:
            out[came[v]].remove(v)
            out[v].add(came[v])
            v = came[v]
    left = {v: sorted(out[v] - {v})[0] for v in range(LEFT)}
    rest = {v: sorted(out[v] - ({left[v]} if v in left else set())) for v in range(F)}
    partner = [[rest[base[p]].pop(0) for p in range(P)] for _ in range(CHUNKS)]
    return partner, left


def t_uses(first):
    uses = [("emb", 0), ("base", 0)] if first else [("tr", -1), ("emb", 0), ("base", 0), ("xT", -2)]
    for c in range(COLS - 1):
        uses += [("base", c + 1)] + ([] if first and c == 0 else [("xT", c - 1)]) + [("tr", c)]
    return uses


T_FIRST, T_LATER, T_END = t_uses(True), t_uses(False), [("tr", -1), ("xT", -2), ("xT", -1)]
BEGIN = -5
END = 6
Z_BEGIN, Z_STEPS = 4, 5


def steps(tile):
    return range(BEGIN if tile is not None else 0, END if isinstance(tile, int) else SLOTS + BEGIN)


def count(tile, per_tile, k):
    return k if tile is None else tile * per_tile + (per_tile + k)


def t_count(tile, use):
    if tile is None:
        return T_FIRST.index(use) + 1
    if use == ("tr", -2):
        return tile * len(T_LATER) + len(T_FIRST)
    uses = T_END if isinstance(tile, int) else T_LATER
    return tile * len(T_LATER) + (len(T_FIRST) + uses.index(use) + 1)


def build(nc, ids, dense3, sel, ident, ones_col, w0a, w0b, w1, wt1, wt1d3, wt2, wt3, b1, b2, tables, out):
    ctx = ExitStack()
    with ctx:
        def sb(name, shape, dt=F32):
            return ctx.enter_context(nc.sbuf_tensor(name, shape, dt))

        def ps(name, shape):
            return ctx.enter_context(nc.psum_tensor(name, shape, F32))

        def sem(name):
            return ctx.enter_context(nc.semaphore(name))

        ids_sb = sb("ids_sb", [P, TILES * F], I32)
        idx = sb("idx", [P, F], I32)
        emb = sb("emb", [P, F * D])
        emb_split = sb("emb_split", [P, SPLIT, D])
        embT = sb("embT", [SPLIT, P, D], F32R)
        sel_r = sb("sel_r", [SPLIT, (CHUNKS + 2) * P], F32R)
        ident_sb = sb("ident_sb", [P, P])
        base_sb = sb("base_sb", [P, 2, 512])
        prod = sb("prod", [P, STEPS, 2, 512])
        prod_hi = sb("prod_hi", [P, STEPS, 2, 512], F32R)
        prod_lo = sb("prod_lo", [P, LAST, 2, 512], F32R)
        w0_hi = sb("w0_hi", [P, CHUNKS + 1, H], F32R)
        w0_lo = sb("w0_lo", [P, CHUNKS, H], F32R)
        w1_sb = sb("w1_sb", [P, F, H])
        x1_sb = sb("x1_sb", [P, 2, 512])
        x1T_hi = sb("x1T_hi", [P, COLS, NG, H], F32R)
        x1T_lo = sb("x1T_lo", [P, COLS, NG, H], F32R)
        e_rows = sb("e_rows", [P, 2, NG, SPLIT])
        e_diag = [sb(f"e_diag{i}", [P, NG, 2, GB, GF], F32R) for i in range(COLS)]
        ones_sb = sb("ones_sb", [P, GB])
        gram_sb = sb("gram_sb", [P, GF, P])
        z1T = sb("z1T", [P, B])
        z2T = sb("z2T", [P, B])
        dense3_r = sb("dense3_r", [LROWS, B], F32R)
        wt1_sb = sb("wt1_sb", [P, 2, M1])
        wt1d3_r = sb("wt1d3_r", [LROWS, M1], F32R)
        z_hi = sb("z_hi", [P, 2, E], F32R)
        z_lo = sb("z_lo", [P, 2, E], F32R)
        wt2_sb = sb("wt2_sb", [P, M1 // P, M2])
        wt3_sb = sb("wt3_sb", [P, M2 // P])
        b1_sb = sb("b1_sb", [P, M1 // P])
        b2_sb = sb("b2_sb", [P, M2 // P])
        y_sb = sb("y_sb", [1, B])
        w0a_sb = prod[:, 0, :, :].rearrange("p a n -> p (a n)")[:, 0:(CHUNKS + 1) * H]
        w0b_sb = prod[:, 1, :, :].rearrange("p a n -> p (a n)")[:, 0:(CHUNKS + 1) * H]
        sel_sb = prod[0:SPLIT, 2, :, :].rearrange("p a n -> p (a n)")
        dense3_sb, wt1d3_sb = prod[0:LROWS, LAST, 0, :], prod[0:LROWS, LAST, 1, :]
        wt1_hi, wt1_lo = prod_hi[:, 0, :, :], prod_lo[:, 0, :, :]
        wt2_hi = prod_hi[:, 1, :, :].rearrange("p a (k n) -> p (a k) n", n=M2)
        wt2_lo = prod_lo[:, 1, :, :].rearrange("p a (k n) -> p (a k) n", n=M2)

        def four_of_e(x):
            return x.rearrange("p s a n -> p (s a n)")[:, 0:4 * E].rearrange("p (k n) -> p k n", n=E)

        h1 = four_of_e(prod[:, 0:2, :, :])
        h1_hi = four_of_e(prod_hi[:, 2:4, :, :])
        h1_lo = e_diag[0][:, :, :, :, :].rearrange("p n s b f -> p (n s b f)")[:, 0:4 * E].rearrange(
            "p (k n) -> p k n", n=E)
        h2 = base_sb[:, :, 0:E]
        h1_late = x1_sb[:, 0, :].rearrange("p (k n) -> p k n", n=P)
        h2_late = x1_sb[:, 1, 0:2 * P].rearrange("p (k n) -> p k n", n=P)

        sel_ps = [ps(f"sel_ps{i}", [P, 2, 512]) for i in range(2)]
        x1_ps = ps("x1_ps", [P, 512])
        t_ps = ps("t_ps", [P, 512])
        gz_ps = [ps(f"gz_ps{i}", [P, 512]) for i in range(2)]
        z_ps = gz_ps[1]

        def emb_ps(q):
            return [gz_ps[0], gz_ps[1], t_ps, gz_ps[0]][q]

        h1_ps = [sel_ps[m // 2][:, m % 2, 0:E] for m in range(M1 // P)]
        h2_ps = [x1_ps[:, 0:E], sel_ps[0][:, 0, 0:E]]
        y_ps = sel_ps[0][0:1, 1, :]
        h1_late_ps, h2_late_ps = sel_ps[1][:, 0, :], sel_ps[1][:, 1, 0:M2]

        ids_in = sem("ids_in")
        consts_in = sem("consts_in")
        w1_in = sem("w1_in")
        tower_in = sem("tower_in")
        idx_ready = sem("idx_ready")
        look_up_begun = sem("look_up_begun")
        looked_up = [sem(f"looked_up{p}") for p in range(PARTS)]
        sel_ready = sem("sel_ready")
        w0_sum = sem("w0_sum")
        w0_hi_done = sem("w0_hi_done")
        w0_ready = sem("w0_ready")
        diag_zero = sem("diag_zero")
        diag_ready = sem("diag_ready")
        emb_hi_done = sem("emb_hi_done")
        emb_lo_done = sem("emb_lo_done")
        emb_turned = sem("emb_turned")
        embT_done = sem("embT_done")
        t_full = sem("t_full")
        xT_hi_done = sem("xT_hi_done")
        t_free = sem("t_free")
        sel_done = sem("sel_done")
        mult_done = sem("mult_done")
        hi_done = sem("hi_done")
        lo_done = sem("lo_done")
        main_done = sem("main_done")
        x1_taken = sem("x1_taken")
        diag_in = [sem(f"diag_in{i}") for i in range(COLS)]
        g_done = sem("g_done")
        g_taken = sem("g_taken")
        z_done = sem("z_done")
        z_taken = sem("z_taken")
        dense_hi_done = sem("dense_hi_done")
        dense_ready = sem("dense_ready")
        z_hi_done = sem("z_hi_done")
        z_ready = sem("z_ready")
        wt_hi_done = sem("wt_hi_done")
        wt_ready = sem("wt_ready")
        h1_ps_done = sem("h1_ps_done")
        h1_hi_done = sem("h1_hi_done")
        h1_lo_done = sem("h1_lo_done")
        h2_ps_done = sem("h2_ps_done")
        h2_done = sem("h2_done")
        h1_late_ps_done = sem("h1_late_ps_done")
        h1_late_done = sem("h1_late_done")
        h2_late_ps_done = sem("h2_late_ps_done")
        h2_late_done = sem("h2_late_done")
        y_ps_done = sem("y_ps_done")
        y_done = sem("y_done")
        y_out = sem("y_out")

        block = ctx.enter_context(nc.Block())

        @block.sync
        def _(sp):
            sp.dma_start(ids_sb[:, :].rearrange("p (t f) -> p t f", f=F),
                         ids.rearrange("(t p) f -> p t f", p=P)).then_inc(ids_in, 16)
            sp.dma_start(sel_sb, sel).then_inc(consts_in, 16)
            sp.dma_start(w0a_sb, w0a).then_inc(consts_in, 16)
            sp.dma_start(w0b_sb, w0b).then_inc(consts_in, 16)
            sp.dma_start(ident_sb[:, :], ident).then_inc(consts_in, 16)
            sp.dma_start(ones_sb[:, :], ones_col).then_inc(consts_in, 16)
            sp.dma_start(dense3_sb, dense3).then_inc(consts_in, 16)
            sp.dma_start(wt1d3_sb, wt1d3).then_inc(consts_in, 16)
            sp.dma_start(w1_sb[:, :, :], w1).then_inc(w1_in, 16)
            sp.dma_start(wt1_sb[:, :, :], wt1[0:2 * P, :].rearrange("(k p) n -> p k n", p=P)).then_inc(tower_in, 16)
            sp.dma_start(wt2_sb[:, :, :], wt2.rearrange("(k p) n -> p k n", p=P)).then_inc(tower_in, 16)
            sp.dma_start(wt3_sb[:, :], wt3).then_inc(tower_in, 16)
            sp.dma_start(b1_sb[:, :], b1).then_inc(tower_in, 16)
            sp.dma_start(b2_sb[:, :], b2).then_inc(tower_in, 16)
            sp.wait_ge(diag_ready, COLS)

            def diagonals(tile):
                for c in range(0 if tile is None else -1, 0 if isinstance(tile, int) else COLS - 1):
                    sp.wait_ge(t_free, t_count(tile, ("tr", c)))
                    for g in range(GB):
                        rows = slice(g * D, (g + 1) * D)
                        sp.dma_start(e_diag[c % COLS][rows, :, :, g, 0:F].bitcast(F32),
                                     e_rows[rows, c % 2, :, :].rearrange("p n (s f) -> p n s f", s=2),
                                     ).then_inc(diag_in[c % COLS], 16)

            diagonals(None)
            with sp.Fori(0, TILES - 1) as u:
                diagonals(u)
            diagonals(TILES - 1)
            sp.wait_ge(y_done, 1)
            sp.dma_start(out, y_sb[:, :]).then_inc(y_out, 16)
            sp.wait_ge(y_out, 16)

        @block.gpsimd
        def _(pool):
            pool.wait_ge(ids_in, 16)

            def look_up(tile):
                for p in range(PARTS):
                    if tile is None:
                        rows_of = ids_sb
                    else:
                        rows_of = idx
                        pool.wait_ge(emb_lo_done, tile * PARTS + (p + 1))
                        nc.gpsimd.tensor_copy(idx[:, p * PF:(p + 1) * PF],
                                              ids_sb[:, bass.ds((tile + 1) * F + p * PF, PF)]).then_inc(idx_ready, 1)
                        pool.wait_ge(idx_ready, tile * PARTS + (p + 1))
                        pool.sem_inc(look_up_begun, 1)
                    for f in range(p * PF, (p + 1) * PF):
                        pool.indirect_dma_start(
                            emb[:, f * D:(f + 1) * D], None, tables[f],
                            bass.IndirectOffsetOnAxis(ap=rows_of[:, f:f + 1], axis=0),
                        ).then_inc(looked_up[p], 16)

            look_up(None)
            with pool.Fori(0, TILES - 1) as u:
                look_up(u)

        @block.tensor
        def _(pe):
            def selector(c):
                return sel_r[:, c * P:(c + 1) * P]

            def samples(b0, n):
                return embT[:, b0:b0 + n, :].rearrange("p b d -> p (b d)")

            def column(c):
                return samples(c % COLS * CB, CB)

            def t_turn(tile, use):
                if tile is not None or use != T_FIRST[0]:
                    pe.wait_ge(t_free, t_count(tile, use) - 1)

            def transpose_emb(tile, q):
                if q == 0:
                    pe.wait_ge(emb_lo_done, count(tile, PARTS, PARTS))
                if q < 2 and tile is not None:
                    pe.wait_ge(g_taken, count(tile, SLOTS, -3 * NG - 1 + q))
                if q == 2:
                    t_turn(tile, ("emb", 0))
                if q == 3:
                    pe.wait_ge(embT_done, count(tile, 3, 1))
                for k in range(4):
                    mm = nc.tensor.transpose(emb_ps(q)[0:SPLIT, k * P:(k + 1) * P],
                                             emb_split[:, :, 4 * q + k], ident_sb[:, :])
                mm.then_inc(t_full if q == 2 else emb_turned, 1)

            def base_rows(tile, c):
                t_turn(tile, ("base", c))
                if tile is None and c == 0:
                    pe.wait_ge(embT_done, 3)
                nc.tensor.matmul(t_ps[:, :], selector(0), column(c), start=True, stop=True).then_inc(t_full, 1)

            def emb_rows(tile, c):
                t_turn(tile, ("tr", c))
                for g in range(NG):
                    b0 = (c % COLS) * CB + g * GB
                    mm = nc.tensor.transpose(
                        t_ps[:, g * SPLIT:(g + 1) * SPLIT],
                        samples(b0, GB).bitcast(F32),
                        ident_sb[0:SPLIT, 0:SPLIT])
                mm.then_inc(t_full, 1)

            def transpose_x1(tile, c):
                t_turn(tile, ("xT", c))
                pe.wait_ge(x1_taken, count(tile, COLS, c + 1))
                for g in range(NG):
                    mm = nc.tensor.transpose(t_ps[:, g * P:(g + 1) * P], x1_sb[:, c % 2, g * P:(g + 1) * P],
                                             ident_sb[:, :])
                mm.then_inc(t_full, 1)

            def partners(tile, n):
                c, s = divmod(n, STEPS)
                if tile is not None or n >= 2:
                    pe.wait_ge(mult_done, count(tile, SLOTS, n - 1))
                if n == 0:
                    pe.wait_ge(t_free, t_count(tile, ("emb", 0)))
                    pe.wait_ge(embT_done, count(tile, 3, 3))
                    if tile is None:
                        pe.wait_ge(sel_ready, 1)
                if s < LAST:
                    for a in range(2):
                        mm = nc.tensor.matmul(sel_ps[s % 2][:, a, :], selector(1 + 2 * s + a), column(c),
                                              start=True, stop=True)
                else:
                    mm = nc.tensor.matmul(sel_ps[s % 2][0:LROWS, 0, :], selector(1 + CHUNKS)[:, 0:LROWS],
                                          column(c), start=True, stop=True)
                mm.then_inc(sel_done, 1)

            def main(tile, n):
                c, s = divmod(n, STEPS)
                if tile is None and n == 0:
                    pe.wait_ge(w0_ready, 1)
                if s == 0 and (tile is not None or c > 0):
                    pe.wait_ge(x1_taken, count(tile, COLS, c))
                pe.wait_ge(lo_done, count(tile, SLOTS, n + 1))
                if s < LAST:
                    for a in range(2):
                        k = 2 * s + a
                        hi, lo = prod_hi[:, s, a, :], prod_lo[:, s, a, :]
                        nc.tensor.matmul(x1_ps[:, :], w0_hi[:, k, :], hi, start=(k == 0), stop=False)
                        nc.tensor.matmul(x1_ps[:, :], w0_hi[:, k, :], lo, start=False, stop=False)
                        mm = nc.tensor.matmul(x1_ps[:, :], w0_lo[:, k, :], hi, start=False, stop=False)
                else:
                    mm = nc.tensor.matmul(x1_ps[:, :], w0_hi[0:LROWS, CHUNKS, :], prod_hi[0:LROWS, s, 0, :],
                                          start=False, stop=True)
                mm.then_inc(main_done, 1)

            def gram(tile, c, g):
                if g == 0:
                    if c != -3:
                        pe.wait_ge(t_free, t_count(tile, ("xT", c)))
                    pe.wait_ge(diag_in[c % COLS], count(tile, 16 * GB, 16 * GB if c >= 0 else 0))
                if tile is not None or g > 1:
                    pe.wait_ge(g_taken, count(tile, SLOTS, NG * c + g - 1))
                if tile is not None and (c, g) == (0, 1):
                    pe.wait_ge(z_taken, 2 * tile + 3)
                o = gz_ps[g % 2][:, 0:GB * GF]
                e_hi = e_diag[c % COLS][:, g, 0, :, :].rearrange("p b f -> p (b f)")
                e_lo = e_diag[c % COLS][:, g, 1, :, :].rearrange("p b f -> p (b f)")
                nc.tensor.matmul(o, x1T_hi[:, c % COLS, g, :], e_hi, start=True, stop=False)
                nc.tensor.matmul(o, x1T_hi[:, c % COLS, g, :], e_lo, start=False, stop=False)
                nc.tensor.matmul(o, x1T_lo[:, c % COLS, g, :], e_hi, start=False, stop=True).then_inc(g_done, 1)

            def layer2(tile, j0, j1):
                if j0 == 0:
                    pe.wait_ge(g_taken, count(tile, SLOTS, 0))
                for j in range(j0, j1):
                    mm = nc.tensor.matmul(z_ps[:, 0:P], w1_sb[:, j, :], gram_sb[:, j, :],
                                          start=(j == 0), stop=(j == F - 1))
                if j1 == F:
                    mm.then_inc(z_done, 1)

            def tower1(m):
                if m == 0:
                    pe.wait_ge(dense_ready, 1)
                    pe.wait_ge(z_ready, 1)
                    pe.wait_ge(wt_ready, 1)
                if m % 2 == 0:
                    pe.wait_ge(mult_done, TILES * SLOTS - 1 + m // 2)
                cols = slice(m * P, (m + 1) * P)
                nc.tensor.matmul(h1_ps[m], wt1d3_r[:, cols], dense3_r[:, 0:E], start=True, stop=False)
                for k in range(2):
                    nc.tensor.matmul(h1_ps[m], wt1_hi[:, k, cols], z_hi[:, k, :], start=False, stop=False)
                    nc.tensor.matmul(h1_ps[m], wt1_hi[:, k, cols], z_lo[:, k, :], start=False, stop=False)
                    mm = nc.tensor.matmul(h1_ps[m], wt1_lo[:, k, cols], z_hi[:, k, :], start=False, stop=(k == 1))
                mm.then_inc(h1_ps_done, 1)

            def tower2(m):
                if m == 0:
                    pe.wait_ge(wt_ready, 2)
                    pe.wait_ge(x1_taken, TILES * COLS)
                cols = slice(m * P, (m + 1) * P)
                for k in range(M1 // P):
                    pe.wait_ge(h1_lo_done, k + 1)
                    nc.tensor.matmul(h2_ps[m], wt2_hi[:, k, cols], h1_hi[:, k, :], start=(k == 0), stop=False)
                    nc.tensor.matmul(h2_ps[m], wt2_hi[:, k, cols], h1_lo[:, k, :], start=False, stop=False)
                    mm = nc.tensor.matmul(h2_ps[m], wt2_lo[:, k, cols], h1_hi[:, k, :], start=False,
                                          stop=(k == M1 // P - 1))
                mm.then_inc(h2_ps_done, 1)

            def do_tile(tile):
                first, last = tile is None, isinstance(tile, int)
                if first:
                    for q in range(4):
                        transpose_emb(tile, q)
                    base_rows(tile, 0)
                    for n in range(3):
                        partners(tile, n)
                for n in steps(tile):
                    c, s = divmod(n, STEPS)
                    if (n + 3 < 0 or not last) and n != -3:
                        partners(tile, n + 3)
                    if n < 0 or not last:
                        main(tile, n)
                    if n == -3 and not last:
                        partners(tile, 0)
                    if n == -4:
                        emb_rows(tile, -1)
                        if not last:
                            for q in range(4):
                                transpose_emb(tile, q)
                    if n == -3 and not last:
                        base_rows(tile, 0)
                    if s == 0 and n >= 0 and not last:
                        base_rows(tile, c + 1)
                    if n in (SLOTS + BEGIN - 1, BEGIN):
                        for g in range(2):
                            gram(tile, *((0, g) if n > 0 else (-4, g + 2)))
                    if n in (-3, -2):
                        for g in range(2):
                            gram(tile, -3, 2 * (n + 3) + g)
                    if 0 <= n < 4 and not first:
                        for i in range(2 * n, 2 * n + 2):
                            gram(tile, i // NG - 2, i % NG)
                    if last and 1 <= n <= M1 // P:
                        tower1(n - 1)
                    if Z_BEGIN <= n < Z_BEGIN + Z_STEPS and not first and not last:
                        j = n - Z_BEGIN
                        layer2(tile, j * F // Z_STEPS, (j + 1) * F // Z_STEPS)
                    if n == -2:
                        transpose_x1(tile, -2)
                    if s == 0 and n >= 0 and not (first and c == 0) and not (last and c > 0):
                        transpose_x1(tile, c - 1)
                    if s == 2 and n >= 0 and not last:
                        emb_rows(tile, c)

            pe.wait_ge(consts_in, 7 * 16)
            do_tile(None)
            pe.wait_ge(w1_in, 16)
            with pe.Fori(0, TILES - 1) as u:
                do_tile(u)
            end = TILES - 1
            do_tile(end)
            layer2(end, 0, F)

            pe.wait_ge(tower_in, 5 * 16)
            for m in range(M2 // P):
                tower2(m)
            pe.wait_ge(z_taken, 2 * TILES + 1)
            for m in range(M1 // P):
                o = h1_late_ps[:, m * P:(m + 1) * P]
                cols = slice(m * P, (m + 1) * P)
                nc.tensor.matmul(o, wt1d3_r[:, cols], dense3_r[:, E:B], start=True, stop=False)
                nc.tensor.matmul(o, wt1_sb[:, 0, cols], z1T[:, E:B], start=False, stop=False)
                mm = nc.tensor.matmul(o, wt1_sb[:, 1, cols], z2T[:, E:B], start=False, stop=True)
            mm.then_inc(h1_late_ps_done, 1)
            for k in range(M2 // P):
                pe.wait_ge(h2_done, k + 1)
                nc.tensor.matmul(y_ps[:, 0:E], wt3_sb[:, k:k + 1], h2[:, k, :],
                                 start=(k == 0), stop=(k == M2 // P - 1))
            for m in range(M2 // P):
                for k in range(M1 // P):
                    pe.wait_ge(h1_late_done, k + 1)
                    mm = nc.tensor.matmul(h2_late_ps[:, m * P:(m + 1) * P], wt2_sb[:, k, m * P:(m + 1) * P],
                                          h1_late[:, k, :], start=(k == 0), stop=(k == M1 // P - 1))
            mm.then_inc(h2_late_ps_done, 1)
            for k in range(M2 // P):
                pe.wait_ge(h2_late_done, k + 1)
                mm = nc.tensor.matmul(y_ps[:, E:B], wt3_sb[:, k:k + 1], h2_late[:, k, :],
                                      start=(k == 0), stop=(k == M2 // P - 1))
            mm.then_inc(y_ps_done, 1)

        @block.scalar
        def _(act):
            def copy(o, i):
                return nc.scalar.activation(o, i, ACT.Copy)

            def split_emb(tile):
                for p in range(PARTS):
                    act.wait_ge(looked_up[p], count(tile, 16 * PF, 16 * PF))
                    fields = slice(p * PF, (p + 1) * PF)
                    copy(emb_split[:, fields, :].bitcast(F32R),
                         emb[:, p * PF * D:(p + 1) * PF * D].rearrange("p (f d) -> p f d", d=D),
                         ).then_inc(emb_hi_done, 1)

            def take_embT(tile, q):
                if q == 2:
                    act.wait_ge(t_full, t_count(tile, ("emb", 0)))
                else:
                    act.wait_ge(emb_turned, count(tile, 3, min(q + 1, 3)))
                done = copy(embT[:, :, 4 * q:4 * q + 4].rearrange("p b d -> p d b"),
                            emb_ps(q)[0:SPLIT, :].rearrange("p (d b) -> p d b", d=4))
                done.then_inc(t_free if q == 2 else embT_done, 1)

            def take_base(tile, c):
                act.wait_ge(t_full, t_count(tile, ("base", c)))
                if tile is not None or c >= 2:
                    act.wait_ge(mult_done, count(tile, SLOTS, STEPS * (c - 1)))
                copy(base_sb[:, c % 2, :], t_ps[:, :]).then_inc(t_free, 1)

            def take_emb_rows(tile, c):
                act.wait_ge(t_full, t_count(tile, ("tr", c)))
                if tile is not None or c > 1:
                    act.wait_ge(diag_in[(c - 2) % COLS], count(tile, 16 * GB, 0 if c <= 1 else 16 * GB))
                copy(e_rows[:, c % 2, :, :].rearrange("p n f -> p (n f)"), t_ps[:, 0:NG * SPLIT]).then_inc(t_free, 1)

            def take_x1T(tile, c):
                act.wait_ge(t_full, t_count(tile, ("xT", c)))
                copy(x1T_hi[:, c % COLS, :, :].rearrange("p n h -> p (n h)"), t_ps[:, :]).then_inc(xT_hi_done, 1)

            def products_hi(tile, n):
                s = n % STEPS
                act.wait_ge(mult_done, count(tile, SLOTS, n + 1))
                if tile is not None or n >= STEPS:
                    act.wait_ge(main_done, count(tile, SLOTS, n - STEPS + 1))
                if s < LAST:
                    copy(prod_hi[:, s, :, :], prod[:, s, :, :]).then_inc(hi_done, 1)
                else:
                    copy(prod_hi[0:LROWS, s, 0, :], prod[0:LROWS, s, 0, :]).then_inc(hi_done, 1)

            def take_x1(tile, c):
                act.wait_ge(main_done, count(tile, SLOTS, STEPS * (c + 1)))
                copy(x1_sb[:, c % 2, :], x1_ps[:, :]).then_inc(x1_taken, 1)

            def take_gram(tile, c, g):
                act.wait_ge(g_done, count(tile, SLOTS, NG * c + g + 1))
                if c == -4 and g == 0:
                    act.wait_ge(z_taken, 2 * tile + 1)
                b0 = (c % COLS) * CB + g * GB
                copy(gram_sb[:, :, b0:b0 + GB].rearrange("p j b -> p b j"),
                     gz_ps[g % 2][:, 0:GB * GF].rearrange("p (b j) -> p b j", b=GB)).then_inc(g_taken, 1)

            def relu(o, i, bias):
                return nc.scalar.activation(o, i, ACT.Relu, bias=bias)

            def z_high():
                act.wait_ge(z_taken, 2 * (TILES - 1) + 1)
                copy(z_hi[:, 0, :], z1T[:, 0:E])
                copy(z_hi[:, 1, :], z2T[:, 0:E]).then_inc(z_hi_done, 1)

            def weights_high(i):
                if i == 0:
                    act.wait_ge(tower_in, 5 * 16)
                act.wait_ge(main_done, TILES * SLOTS - 3 + i)
                copy([wt1_hi, wt2_hi][i], [wt1_sb, wt2_sb][i][:, :, :]).then_inc(wt_hi_done, 1)

            def take_h1(m):
                if m == 0:
                    act.wait_ge(main_done, TILES * SLOTS)
                    act.wait_ge(lo_done, TILES * SLOTS)
                act.wait_ge(h1_ps_done, m + 1)
                relu(h1[:, m, :], h1_ps[m], b1_sb[:, m:m + 1])
                relu(h1_hi[:, m, :], h1_ps[m], b1_sb[:, m:m + 1]).then_inc(h1_hi_done, 1)

            def do_tile(tile):
                first, last = tile is None, isinstance(tile, int)
                if first:
                    split_emb(tile)
                    for q in range(4):
                        take_embT(tile, q)
                    take_base(tile, 0)
                    products_hi(tile, 0)
                for n in steps(tile):
                    c, s = divmod(n, STEPS)
                    if n + 1 < 0 or not last:
                        products_hi(tile, n + 1)
                    if n == BEGIN:
                        for g in range(2):
                            take_gram(tile, -4, g)
                    if n in (-2, -1):
                        for g in range(2):
                            take_gram(tile, -3, 2 * (n + 2) + g)
                    if 1 <= n < 5 and not first:
                        for i in range(2 * n - 2, 2 * n):
                            take_gram(tile, i // NG - 2, i % NG)
                    if n == -4:
                        take_emb_rows(tile, -1)
                        if not last:
                            for q in range(4):
                                take_embT(tile, q)
                    if n == -1:
                        take_x1T(tile, -2)
                    if n == -3 and not last:
                        take_base(tile, 0)
                    if s == 0 and n >= 0 and not last:
                        take_base(tile, c + 1)
                    if s == 1 and n > 0 and not (first and c == 0) and not (last and c > 0):
                        take_x1T(tile, c - 1)
                    if s == 3 and n != -1 and not (last and n > 0):
                        take_emb_rows(tile, c)
                    if s == 3 and (n < 0 or not last):
                        take_x1(tile, c)
                    if n == BEGIN:
                        for g in range(2, NG):
                            take_gram(tile, -4, g)
                    if n == BEGIN and not last:
                        split_emb(tile)
                    if last and n == -2:
                        weights_high(0)
                    if last and n == 0:
                        z_high()
                    if last and 2 <= n < 2 + M1 // P:
                        take_h1(n - 2)

            act.wait_ge(consts_in, 7 * 16)
            copy(dense3_r[:, :], dense3_sb)
            copy(wt1d3_r[:, :], wt1d3_sb).then_inc(dense_hi_done, 1)
            act.wait_ge(w0_sum, 1)
            copy(w0_hi[:, :, :].rearrange("p k h -> p (k h)"), w0a_sb).then_inc(w0_hi_done, 1)
            do_tile(None)
            with act.Fori(0, TILES - 1) as u:
                do_tile(u)
            end = TILES - 1
            do_tile(end)

            weights_high(1)
            for m in range(M2 // P):
                act.wait_ge(h2_ps_done, m + 1)
                relu(h2[:, m, :], h2_ps[m], b2_sb[:, m:m + 1]).then_inc(h2_done, 1)
            act.wait_ge(h1_late_ps_done, 1)
            for m in range(M1 // P):
                relu(h1_late[:, m, :], h1_late_ps[:, m * P:(m + 1) * P], b1_sb[:, m:m + 1]).then_inc(h1_late_done, 1)
            act.wait_ge(h2_late_ps_done, 1)
            for m in range(M2 // P):
                relu(h2_late[:, m, :], h2_late_ps[:, m * P:(m + 1) * P], b2_sb[:, m:m + 1]).then_inc(h2_late_done, 1)
            act.wait_ge(y_ps_done, 1)
            copy(y_sb[:, :], y_ps).then_inc(y_done, 1)

        @block.vector
        def _(dve):
            def subtract(o, whole, hi):
                return nc.vector.tensor_tensor(o, whole, hi, ALU.subtract)

            def split_emb(tile):
                for p in range(PARTS):
                    dve.wait_ge(emb_hi_done, count(tile, PARTS, p + 1))
                    subtract(emb_split[:, F + p * PF:F + (p + 1) * PF, :],
                             emb[:, p * PF * D:(p + 1) * PF * D].rearrange("p (f d) -> p f d", d=D),
                             emb_split[:, p * PF:(p + 1) * PF, :]).then_inc(emb_lo_done, 1)

            def multiply(tile, n):
                c, s = divmod(n, STEPS)
                dve.wait_ge(sel_done, count(tile, SLOTS, n + 1))
                if s == 0:
                    dve.wait_ge(t_free, t_count(tile, ("base", c)))
                if tile is not None or n >= STEPS:
                    dve.wait_ge(hi_done, count(tile, SLOTS, n - STEPS + 1))
                if s < LAST:
                    base = base_sb[:, c % 2, :].unsqueeze(1).to_broadcast([P, 2, 512])
                    nc.vector.tensor_tensor(prod[:, s, :, :], sel_ps[s % 2][:, :, :], base,
                                            ALU.mult).then_inc(mult_done, 1)
                else:
                    nc.vector.tensor_tensor(prod[0:LROWS, s, 0, :], sel_ps[s % 2][0:LROWS, 0, :],
                                            base_sb[0:LROWS, c % 2, :], ALU.mult).then_inc(mult_done, 1)

            def products_lo(tile, n):
                s = n % STEPS
                dve.wait_ge(hi_done, count(tile, SLOTS, n + 1))
                if tile is not None or n >= STEPS:
                    dve.wait_ge(main_done, count(tile, SLOTS, n - STEPS + 1))
                if s < LAST:
                    subtract(prod_lo[:, s, :, :], prod[:, s, :, :],
                             prod_hi[:, s, :, :].bitcast(F32)).then_inc(lo_done, 1)
                else:
                    subtract(prod_hi[32:64, s, 0, :], prod[32:64, s, 0, :],
                             prod_hi[32:64, s, 0, :].bitcast(F32)).then_inc(lo_done, 1)

            def take_x1T(tile, c):
                dve.wait_ge(xT_hi_done, count(tile, COLS, c + 1))
                subtract(x1T_lo[:, c % COLS, :, :].rearrange("p n h -> p (n h)"), t_ps[:, :],
                         x1T_hi[:, c % COLS, :, :].rearrange("p n h -> p (n h)").bitcast(F32)).then_inc(t_free, 1)

            def take_z(tile):
                dve.wait_ge(g_taken, count(tile, SLOTS, 0))
                nc.vector.tensor_copy(z1T[:, bass.ds(tile * P, P)], gram_sb[:, F, :]).then_inc(z_taken, 1)
                dve.wait_ge(z_done, tile + 1)
                nc.vector.tensor_copy(z2T[:, bass.ds(tile * P, P)], z_ps[:, 0:P]).then_inc(z_taken, 1)

            def z_low():
                dve.wait_ge(z_hi_done, 1)
                subtract(z_lo[:, 0, :], z1T[:, 0:E], z_hi[:, 0, :].bitcast(F32))
                subtract(z_lo[:, 1, :], z2T[:, 0:E], z_hi[:, 1, :].bitcast(F32)).then_inc(z_ready, 1)

            def weights_low(i):
                dve.wait_ge(wt_hi_done, i + 1)
                subtract([wt1_lo, wt2_lo][i], [wt1_sb, wt2_sb][i][:, :, :],
                         [wt1_hi, wt2_hi][i].bitcast(F32)).then_inc(wt_ready, 1)

            def h1_low(m):
                dve.wait_ge(h1_hi_done, m + 1)
                subtract(h1_lo[:, m, :], h1[:, m, :], h1_hi[:, m, :].bitcast(F32)).then_inc(h1_lo_done, 1)

            def do_tile(tile):
                first, last = tile is None, isinstance(tile, int)
                if first:
                    split_emb(tile)
                    multiply(tile, 0)
                    multiply(tile, 1)
                    products_lo(tile, 0)
                for n in steps(tile):
                    c, s = divmod(n, STEPS)
                    if n + 2 < 0 or not last:
                        multiply(tile, n + 2)
                    if n + 1 < 0 or not last:
                        products_lo(tile, n + 1)
                    if n == BEGIN and not last:
                        split_emb(tile)
                    if n == -1:
                        take_x1T(tile, -2)
                    if s == 1 and n > 0 and not (first and c == 0) and not (last and c > 0):
                        take_x1T(tile, c - 1)
                    if n == Z_BEGIN + Z_STEPS and not first:
                        take_z(tile)
                    if last and n == 0:
                        weights_low(0)
                        z_low()
                    if last and 2 <= n < 2 + M1 // P:
                        h1_low(n - 2)

            for i in range(COLS):
                nc.vector.memset(e_diag[i][:, :, :, :, :].bitcast(F32), 0.0).then_inc(diag_zero, 1)
            dve.wait_ge(consts_in, 7 * 16)
            nc.vector.tensor_copy(sel_r[:, :], sel_sb).then_inc(sel_ready, 1)
            nc.vector.tensor_tensor(w0a_sb, w0a_sb, w0b_sb, ALU.add).then_inc(w0_sum, 1)
            dve.wait_ge(dense_hi_done, 1)
            subtract(dense3_r[32:64, :], dense3_sb[32:64, :], dense3_r[32:64, :].bitcast(F32))
            subtract(wt1d3_r[64:96, :], wt1d3_sb[64:96, :],
                     wt1d3_r[64:96, :].bitcast(F32)).then_inc(dense_ready, 1)
            dve.wait_ge(diag_zero, COLS)
            for i in range(COLS):
                for g in range(NG):
                    last = nc.vector.tensor_copy(e_diag[i][:, g, 0, :, F], ones_sb[:, :])
                last.then_inc(diag_ready, 1)
            dve.wait_ge(w0_hi_done, 1)
            n = CHUNKS * H
            subtract(w0_lo[:, :, :].rearrange("p k h -> p (k h)"), w0a_sb[:, 0:n],
                     w0_hi[:, 0:CHUNKS, :].rearrange("p k h -> p (k h)").bitcast(F32)).then_inc(z_taken, 1)
            subtract(w0_hi[64:96, CHUNKS, :], w0a_sb[64:96, n:n + H],
                     w0_hi[64:96, CHUNKS, :].bitcast(F32)).then_inc(w0_ready, 1)
            do_tile(None)
            with dve.Fori(0, TILES - 1) as u:
                do_tile(u)
            end = TILES - 1
            do_tile(end)
            weights_low(1)
            take_z(end)


def kernel(**inputs):
    import concourse.bacc as bacc
    from concourse.bass_utils import run_bass_kernel_spmd

    partner, left = pair_tables()
    base = base_fields()

    sel = np.zeros((SPLIT, CHUNKS + 2, P), np.float32)
    rows = np.arange(P)
    left_rows = [(r + v, v, w) for r in (0, 32, 64) for v, w in left.items()]
    for s in range(2):
        sel[s * F + np.array(base), 0, rows] = 1
        for c in range(CHUNKS):
            sel[s * F + np.array(partner[c]), 1 + c, rows] = 1
        for p, _, w in left_rows:
            sel[s * F + w, 1 + CHUNKS, p] = 1

    w0 = np.asarray(inputs["L0_rec_W0"])
    w0a = np.zeros((P, CHUNKS + 1, H), w0.dtype)
    w0b = np.zeros((P, CHUNKS + 1, H), w0.dtype)
    for p, c, i, j in ([(p, c, base[p], partner[c][p]) for c in range(CHUNKS) for p in range(P)]
                       + [(p, CHUNKS, i, j) for p, i, j in left_rows]):
        w0a[p, c] = w0[:, i * F + j]
        if i != j:
            w0b[p, c] = w0[:, j * F + i]

    dense, wt1 = np.asarray(inputs["dense_ctx"]), np.asarray(inputs["W_top1"])
    dense3, wt1d3 = np.zeros((LROWS, B), dense.dtype), np.zeros((LROWS, M1), wt1.dtype)
    for r in (0, 32, 64):
        dense3[r:r + DENSE] = dense.T
        wt1d3[r:r + DENSE] = wt1[2 * P:]

    w1 = np.asarray(inputs["L0_rec_W1"]).reshape(H, H, F).transpose(1, 2, 0)
    arrays = {
        "ids": np.asarray(inputs["ids"]),
        "dense3": dense3,
        "sel": sel.reshape(SPLIT, -1),
        "ident": np.eye(P, dtype=np.float32),
        "ones_col": (np.arange(P)[:, None] // D == np.arange(GB)[None, :]).astype(np.float32),
        "w0a": w0a.reshape(P, -1),
        "w0b": w0b.reshape(P, -1),
        "w1": w1,
        "wt1": wt1,
        "wt1d3": wt1d3,
        "wt2": np.asarray(inputs["W_top2"]),
        "wt3": np.asarray(inputs["W_top3"]).reshape(M2 // P, P).T,
        "b1": np.asarray(inputs["b_top1"]).reshape(M1 // P, P).T,
        "b2": np.asarray(inputs["b_top2"]).reshape(M2 // P, P).T,
    }
    for f in range(F):
        arrays[f"tbl_{f}"] = np.asarray(inputs[f"tbl_{f}"])
    arrays = {n: np.ascontiguousarray(a) for n, a in arrays.items()}

    nc = bacc.Bacc("TRN2", target_bir_lowering=False, num_devices=1)
    aps = {n: nc.dram_tensor(f"{n}_dram", a.shape, mybir.dt.from_np(a.dtype), kind="ExternalInput").ap()
           for n, a in arrays.items()}
    out = nc.dram_tensor("y_dram", (1, B), F32, kind="ExternalOutput").ap()
    tables = [aps.pop(f"tbl_{f}") for f in range(F)]
    build(nc, tables=tables, out=out, **aps)
    r = run_bass_kernel_spmd(nc, [{f"{n}_dram": a for n, a in arrays.items()}], core_ids=[0])
    return r.results[0]["y_dram"].reshape(B, 1)
```
